# Optimizing a Trainium2 kernel written in Bass

```python
import numpy as np
import jax
import jax.numpy as jnp

def _softmax(x, axis=-1):
    return jax.nn.softmax(x, axis=axis)

def _gelu(x):
    return jax.nn.gelu(x, approximate=True)

def _silu(x):
    return jax.nn.silu(x)

def _sigmoid(x):
    return jax.nn.sigmoid(x)

def _layernorm(x, axis=-1, eps=1e-05):
    m = jnp.mean(x, axis=axis, keepdims=True)
    v = jnp.var(x, axis=axis, keepdims=True)
    return (x - m) / jnp.sqrt(v + eps)

def _scatter_add(tgt, idx, src, axis=0):
    return tgt.at[idx].add(src)

def _segment_sum(src, seg, n):
    return jax.ops.segment_sum(src, seg, n)
kernel_name = 'mk_adj_preln_d2_adj_r2_c83c4f'

def setup_inputs(seed: int=0):
    np.random.seed(seed)
    _w = jnp.asarray

    def _rec_inputs():
        import jax
        import jax.numpy as jnp
        _gk = jax.random.key(seed)
        x = -0.0002928 + 1 * jax.random.normal(jax.random.fold_in(_gk, 1), (4096, 256), jnp.float32)
        _w = (1.0 + jnp.arange(4096, dtype=jnp.float32)) ** (-0.5)
        _w = _w / _w.mean()
        _pij = jnp.clip(0.000976562 * _w[:, None] * _w[None, :], 0.0, 1.0)
        _a = jax.random.uniform(jax.random.fold_in(_gk, 2), (4096, 4096)) < _pij
        _a = jnp.logical_or(_a, jnp.eye(4096, dtype=bool))
        _af = _a.astype(jnp.float32)
        _af = _af * jax.random.uniform(jax.random.fold_in(_gk, 3), (4096, 4096), jnp.float32, 0.05, 1)
        adj = _af
        return (x, adj)
    x, adj = _rec_inputs()

    def _L0_gnn_setup():
        import jax, jax.numpy as jnp
        import numpy as np
        N, IN_F, OUT_F = (4096, 256, 256)
        HID = OUT_F // 2
        key = jax.random.key(seed)
        ks = jax.random.split(key, 6)
        x = jax.random.normal(ks[0], (N, IN_F), dtype=jnp.float32)
        adj = jax.random.uniform(ks[1], (N, N), dtype=jnp.float32)
        W1 = jax.random.normal(ks[2], (HID, IN_F), dtype=jnp.float32) * np.sqrt(2.0 / IN_F)
        b1 = jnp.zeros((HID,), dtype=jnp.float32)
        W2 = jax.random.normal(ks[3], (OUT_F, HID), dtype=jnp.float32) * np.sqrt(2.0 / HID)
        b2 = jnp.zeros((OUT_F,), dtype=jnp.float32)
        return {'x': x, 'adj': adj, 'W1': W1, 'b1': b1, 'W2': W2, 'b2': b2}
    _L0_gnn_all = _L0_gnn_setup()
    _L0_gnn_in = {k: v for k, v in _L0_gnn_all.items() if k in ('W1', 'b1', 'W2', 'b2')}
    del _L0_gnn_all

    def _L1_gnn_setup():
        import jax, jax.numpy as jnp
        import numpy as np
        N = 4096
        DIN = 256
        DOUT = 256
        key = jax.random.key(seed)
        k1, k2, k3 = jax.random.split(key, 3)
        x = jax.random.normal(k1, (N, DIN), dtype=jnp.float32)
        adj = jax.random.uniform(k2, (N, N), dtype=jnp.float32)
        W = jax.random.normal(k3, (DIN, DOUT), dtype=jnp.float32) * (1.0 / np.sqrt(DIN))
        b = jnp.zeros((DOUT,), dtype=jnp.float32)
        return {'x': x, 'adj': adj, 'W': W, 'b': b}
    _L1_gnn_all = _L1_gnn_setup()
    _L1_gnn_in = {k: v for k, v in _L1_gnn_all.items() if k in ('W', 'b')}
    del _L1_gnn_all
    return {'x': x, 'adj': adj, 'L0_gnn_W1': _L0_gnn_in['W1'], 'L0_gnn_b1': _L0_gnn_in['b1'], 'L0_gnn_W2': _L0_gnn_in['W2'], 'L0_gnn_b2': _L0_gnn_in['b2'], 'L1_gnn_W': _L1_gnn_in['W'], 'L1_gnn_b': _L1_gnn_in['b']}

def reference(x, adj, L0_gnn_W1, L0_gnn_b1, L0_gnn_W2, L0_gnn_b2, L1_gnn_W, L1_gnn_b):
    import jax
    import jax.numpy as jnp

    def _L0_gnn_ref(x, adj, W1, b1, W2, b2):
        import jax, jax.numpy as jnp
        import numpy as np
        N, IN_F, OUT_F = (4096, 256, 256)
        HID = OUT_F // 2
        h = x @ W1.T + b1
        h = h @ W2.T + b2
        A = adj + jnp.eye(adj.shape[0], dtype=adj.dtype)
        rowsum = A.sum(axis=1)
        r_inv_sqrt = jnp.power(rowsum, -0.5)
        r_inv_sqrt = jnp.where(jnp.isinf(r_inv_sqrt), 0.0, r_inv_sqrt)
        A = r_inv_sqrt[:, None] * A * r_inv_sqrt[None, :]
        return A.astype(jnp.float32) @ h.astype(jnp.float32)

    def _L1_gnn_ref(x, adj, W, b):
        import jax, jax.numpy as jnp
        import numpy as np
        N = 4096
        DIN = 256
        DOUT = 256
        rowsum = adj.sum(axis=1)
        d_inv_sqrt = jnp.where(rowsum > 0, rowsum ** (-0.5), 0.0)
        normalized_adj = d_inv_sqrt[:, None] * adj * d_inv_sqrt[None, :]
        support = normalized_adj @ x
        out = support @ W + b
        return jax.nn.relu(out)
    h = jnp.maximum(_layernorm(x, axis=-1), 0.0)
    x = x + _L0_gnn_ref(h, adj, L0_gnn_W1, L0_gnn_b1, L0_gnn_W2, L0_gnn_b2)
    h = jnp.maximum(_layernorm(x, axis=-1), 0.0)
    x = x + _L1_gnn_ref(h, adj, L1_gnn_W, L1_gnn_b)
    return x

_drawn_inputs = setup_inputs


def setup_inputs(seed=0):
    import zlib

    import numpy as np

    out = dict(_drawn_inputs(seed))
    spreads = {'L0_gnn_b1': (0.0, 0.1), 'L0_gnn_b2': (0.0, 0.1), 'L1_gnn_b': (0.0, 0.1)}
    factors = {}
    for name, (base, spread) in spreads.items():
        noise = np.random.default_rng([zlib.crc32(name.encode()), seed]).standard_normal(out[name].shape)
        drawn = base * np.exp(spread * noise) if base else spread * noise
        out[name] = jnp.asarray(drawn.astype(out[name].dtype))
    for name, factor in factors.items():
        out[name] = (out[name] * factor).astype(out[name].dtype)
    return out
```

```python
from contextlib import ExitStack

import concourse.bass as bass
from concourse import mybir

P = 128
F32 = mybir.dt.float32
F32R = mybir.dt.float32r
ALU = mybir.AluOpType
ACT = mybir.ActivationFunctionType
AX = mybir.AxisListType
LN_EPS = 1e-5
TINY = 1e-30


def gnn_kernel(nc, x, adj, W1, b1, W2, b2, W, b, out):
    N, DF = x.shape
    HID = W1.shape[0]
    T = N // P
    KF = DF // P
    S = 4
    MR = T // S
    SW = 1024
    PC = N // SW
    QW = 512
    QS = SW // QW
    JQ = QW // P
    STR = PC * S
    QUADS = STR * QS
    SLOTS = 8
    RING = 4
    AHEAD = 3
    UW = HID + 2
    FREE_Y = 2

    with ExitStack() as ctx:
        def sb(name, shape, dt=F32):
            return ctx.enter_context(nc.sbuf_tensor(name, shape, dt))

        def sem(name):
            return ctx.enter_context(nc.semaphore(name))

        strips = sb("strips", [P, SLOTS, SW])
        hi = sb("hi", [P, RING, QW], F32R)
        lo = sb("lo", [P, RING, QW], F32R)
        xs = sb("xs", [P, T, DF])
        U = sb("U", [P, T, 2, UW], F32R)
        Y = sb("Y", [P, T, 2, DF], F32R)
        ident = sb("ident", [P, P])
        ident_r = sb("ident_r", [P, P], F32R)
        w_in = sb("w_in", [P, 2, DF])
        W1T = sb("W1T", [P, KF, HID])
        W2T = sb("W2T", [P, DF])
        Wm = sb("Wm", [P, KF, DF])
        b1_all = sb("b1_all", [P, HID])
        b2_all = sb("b2_all", [P, DF])
        b_all = sb("b_all", [P, DF])
        d1 = sb("d1", [P, T])
        d2 = sb("d2", [P, T])
        expo = sb("expo", [P, 4])
        sums = sb("sums", [P, 2, 2])
        stats = sb("stats", [P, 2, 6])
        mv = sb("mv", [P, 2, 2])
        rs = sb("rs", [P, 4])
        mask = sb("mask", [P, 4])
        lnp = sb("lnp", [P, 4])
        ln_scale = sb("ln_scale", [P, 4])
        ln_bias = sb("ln_bias", [P, 4])
        h = sb("h", [P, 2, DF])
        hT = sb("hT", [P, 2, DF])
        ut = sb("ut", [P, 2, UW])
        us = sb("us", [P, 2, UW])
        accb = sb("accb", [P, 2, DF])
        agg = sb("agg", [P, S, DF])
        aggT = sb("aggT", [P, 2, DF])
        ot = sb("ot", [P, 4, DF])

        ps = ctx.enter_context(nc.psum_tensor("ps", [P, 8, 512], F32))

        def acc(s):
            return ps[:, s, :]

        def tbank(q):
            return ps[:, 4 + q % 4, :]

        const_in = sem("const_in")
        x_in = sem("x_in")
        ident_ok = sem("ident_ok")
        ident_r_ok = sem("ident_r_ok")
        wT_ps = sem("wT_ps")
        wT_ok = sem("wT_ok")
        row_in = [sem(f"row_in{i}") for i in range(2)]
        strip_in = [sem(f"strip_in{i}") for i in range(SLOTS)]
        sum_act = sem("sum_act")
        sum_dve = sem("sum_dve")
        stats_ok = sem("stats_ok")
        ln_ok = sem("ln_ok")
        h_ok = sem("h_ok")
        hT_ps = sem("hT_ps")
        hT_ok = sem("hT_ok")
        u_ps = sem("u_ps")
        deg_ok = sem("deg_ok")
        U_ok = sem("U_ok")
        quad_T = sem("quad_T")
        hi_ok = sem("hi_ok")
        lo_ok = sem("lo_ok")
        quad_M = sem("quad_M")
        accb_ok = sem("accb_ok")
        agg_ok = sem("agg_ok")
        agg_ps = sem("agg_ps")
        aggT_ok = sem("aggT_ok")
        fin_ps = sem("fin_ps")
        x1_ok = sem("x1_ok")
        fin_read = sem("fin_read")
        y_ok = sem("y_ok")
        Y_ok = sem("Y_ok")
        out_ok = sem("out_ok")
        out_st = [sem(f"out_st{i}") for i in range(4)]
        dve_step = sem("dve_step")
        pool_step = sem("pool_step")

        waited = sem("waited")

        block = ctx.enter_context(nc.Block())

        def wait_apart(eng, s, n):
            eng.wait_ge(s, n)
            eng.sem_inc(waited, 1)

        class Steps:

            def __init__(self, eng, s):
                self.eng, self.s, self.n = eng, s, 0

            def __call__(self, ins):
                self.n += 1
                ins.then_inc(self.s, 1)
                self.eng.wait_ge(self.s, self.n)

        def macro_rows(eng, body, first, last):
            lo_, hi_ = 0, MR
            if first:
                body(0, True, False)
                lo_ = 1
            if last:
                hi_ = MR - 1
            with eng.Fori(lo_, hi_) as R:
                body(R, False, False)
            if last:
                body(MR - 1, False, True)

        @block.sync
        def _(sp):
            sp.dma_start(w_in[:, 0, :], W1).then_inc(const_in, 16)
            sp.dma_start(w_in[:, 1, :].rearrange("p (k h) -> p k h", k=KF),
                         W2.rearrange("(k p) h -> p k h", p=P)).then_inc(const_in, 16)
            sp.dma_start(Wm[:, :, :], W.rearrange("(k p) f -> p k f", p=P)).then_inc(const_in, 16)
            for dst, src in ((b1_all, b1), (b2_all, b2), (b_all, b)):
                sp.dma_start(dst[:, :], src.rearrange("(a n) -> a n", a=1).to_broadcast([P, src.shape[0]])
                             ).then_inc(const_in, 16)
            sp.dma_start(xs[:, :, :], x.rearrange("(t p) f -> p t f", p=P)).then_inc(x_in, 16)

            def load_row(r, slot):
                sp.dma_start(strips[:, slot * 4:slot * 4 + 4, :],
                             adj[bass.ds(r * P, P), :].rearrange("p (c n) -> p c n", c=PC)
                             ).then_inc(row_in[slot], 16)

            for slot in range(2):
                load_row(slot, slot)
            with sp.Fori(1, T // 2) as i:
                for slot in range(2):
                    sp.wait_ge(sum_act, 2 * i - 1 + slot)
                    sp.wait_ge(sum_dve, 2 * i - 1 + slot)
                    load_row(2 * i + slot, slot)

            def layer_loads(layer):
                def body(R, first, last):
                    for c in range(PC):
                        for s in range(S):
                            g = c * S + s
                            slot = g % SLOTS
                            if layer == 0 and first and g < SLOTS:
                                sp.wait_ge(sum_act, T - 1 + g // 4)
                                sp.wait_ge(sum_dve, T - 1 + g // 4)
                            else:
                                sp.wait_ge(quad_T, (layer * MR + R) * QUADS + (g - SLOTS + 1) * QS)
                            sp.dma_start(strips[:, slot, :],
                                         adj[bass.ds((R * S + s) * P, P), c * SW:(c + 1) * SW]
                                         ).then_inc(strip_in[slot], 16)
                            if layer == 1 and not first and c == PC - 1:
                                store(R - 1, s)
                return body

            def store(R, s):
                sp.wait_ge(out_ok, R * S + s + 1)
                sp.dma_start(out[bass.ds((R * S + s) * P, P), :], ot[:, s, :]).then_inc(out_st[s], 16)

            macro_rows(sp, layer_loads(0), True, False)
            macro_rows(sp, layer_loads(1), True, False)
            for s in range(S):
                store(MR - 1, s)
            for s in range(S):
                sp.wait_ge(out_st[s], 16 * MR)

        @block.gpsimd
        def _(pool):
            step = Steps(pool, pool_step)
            nc.gpsimd.memset(expo[:, :], -0.5)
            step(nc.gpsimd.memset(ident[:, :], 0.0))
            nc.gpsimd.affine_select(out=ident[:, :], in_=ident[:, :], compare_op=ALU.not_equal, fill=1.0,
                                    base=0, pattern=[[-1, P]], channel_multiplier=1).then_inc(ident_ok, 1)
            pool.wait_ge(ident_ok, 1)
            nc.gpsimd.tensor_copy(ident_r[:, :], ident[:, :]).then_inc(ident_r_ok, 1)
            base = step.n

            def norm(k, seq, n, after=None):
                def st(ins):
                    ins.then_inc(pool_step, 1)
                    seq[0] = seq[0] + 1
                    wait_apart(pool, pool_step, seq[0])
                wait_apart(pool, stats_ok, n + 1)
                st(nc.gpsimd.tensor_scalar(lnp[:, 0:1], mv[:, k, 1:2], LN_EPS, None, ALU.add))
                st(nc.gpsimd.tensor_tensor(lnp[:, 1:2], lnp[:, 0:1], expo[:, 0:1], ALU.pow))
                if after is not None:
                    st(nc.gpsimd.tensor_tensor(lnp[:, 2:3], lnp[:, 1:2], after, ALU.mult))
                    r = lnp[:, 2:3]
                else:
                    r = lnp[:, 1:2]
                nc.gpsimd.tensor_copy(ln_scale[:, k:k + 1], r)
                nc.gpsimd.tensor_scalar(ln_bias[:, k:k + 1], mv[:, k, 0:1], r, -1.0, ALU.mult, ALU.mult
                                        ).then_inc(ln_ok, 1)

            PER_TILE = 7

            with pool.Fori(0, T // 2) as i:
                for k in range(2):
                    r = 2 * i + k
                    seq = [base + PER_TILE * r]

                    def st(ins):
                        ins.then_inc(pool_step, 1)
                        seq[0] = seq[0] + 1
                        wait_apart(pool, pool_step, seq[0])

                    norm(k, seq, r)
                    pool.wait_ge(sum_act, r + 1)
                    pool.wait_ge(sum_dve, r + 1)
                    st(nc.gpsimd.tensor_tensor(rs[:, 0:1], sums[:, k, 0:1], sums[:, k, 1:2], ALU.add))
                    st(nc.gpsimd.tensor_scalar(rs[:, 1:2], rs[:, 0:1], 1.0, None, ALU.add))
                    nc.gpsimd.tensor_scalar(mask[:, 0:2], rs[:, 0:2], 0.0, None, ALU.is_gt)
                    st(nc.gpsimd.tensor_scalar(rs[:, 2:4], rs[:, 0:2], TINY, None, ALU.max))
                    st(nc.gpsimd.tensor_tensor(mask[:, 2:4], rs[:, 2:4], expo[:, 0:2], ALU.pow))
                    nc.gpsimd.tensor_tensor(d2[:, bass.ds(r, 1)], mask[:, 2:3], mask[:, 0:1], ALU.mult)
                    st(nc.gpsimd.tensor_tensor(d1[:, bass.ds(r, 1)], mask[:, 3:4], mask[:, 1:2], ALU.mult))
                    nc.gpsimd.sem_inc(deg_ok, 1)
            base += PER_TILE * T
            nc.gpsimd.sem_inc(Y_ok, FREE_Y)

            with pool.Fori(0, MR) as R:
                for s in range(S):
                    r = R * S + s
                    seq = [base + 4 * r]
                    norm(s % 2, seq, r + T, after=d2[:, bass.ds(r, 1)])
                    wait_apart(pool, y_ok, r + 1)
                    nc.gpsimd.tensor_copy(Y[:, r, 0, :], h[:, s % 2, :]).then_inc(pool_step, 1)
                    wait_apart(pool, pool_step, seq[0] + 1)
                    nc.gpsimd.tensor_tensor(Y[:, r, 1, :], h[:, s % 2, :], Y[:, r, 0, :].bitcast(F32),
                                            ALU.subtract).then_inc(Y_ok, 1)

        @block.scalar
        def _(act):
            act.wait_ge(wT_ps, 1)
            nc.scalar.activation(W1T[:, :, :].rearrange("p k h -> p (k h)"), ps[:, 0, 0:KF * HID], ACT.Copy)
            nc.scalar.activation(W2T[:, :], ps[:, 1, 0:DF], ACT.Copy).then_inc(wT_ok, 1)

            with act.Fori(0, T // 2) as i:
                for k in range(2):
                    r = 2 * i + k
                    act.wait_ge(ln_ok, r + 1)
                    nc.scalar.activation(h[:, k, :], xs[:, r, :], ACT.Relu, bias=ln_bias[:, k:k + 1],
                                         scale=ln_scale[:, k:k + 1]).then_inc(h_ok, 1)
                    act.wait_ge(row_in[k], 16 * (i + 1))
                    half = strips[:, 4 * k:4 * k + 2, :].rearrange("p a n -> p (a n)")
                    nc.scalar.activation(half, half, ACT.Copy, accum_out=sums[:, k, 0:1]).then_inc(sum_act, 1)
                    act.wait_ge(hT_ps, r + 1)
                    nc.scalar.activation(hT[:, k, :], ps[:, k, 0:DF], ACT.Copy).then_inc(hT_ok, 1)

            def evac(layer, R, s):
                n = (layer * MR + R) * S + s
                w = DF if layer else UW
                deg = (d2 if layer else d1)[:, bass.ds(R * S + s, 1)]
                act.wait_ge(quad_M, (layer * MR + R) * QUADS + ((PC - 1) * S + s + 1) * QS)
                if not (isinstance(n, int) and n < 2):
                    act.wait_ge(agg_ok, n - 1)
                nc.scalar.activation(accb[:, s % 2, 0:w], acc(s)[:, w:2 * w], ACT.Copy, scale=deg
                                     ).then_inc(accb_ok, 1)

            def copy_T(layer, R, s):
                n = (layer * MR + R) * S + s
                act.wait_ge(agg_ps, n + 1)
                w = DF if layer else HID
                nc.scalar.activation(aggT[:, s % 2, 0:w], acc(s)[:, 0:w], ACT.Copy).then_inc(aggT_ok, 1)

            def make_y(R, s):
                n = R * S + s
                act.wait_ge(ln_ok, T + n + 1)
                act.wait_ge(Y_ok, n - 1 + FREE_Y)
                nc.scalar.activation(h[:, s % 2, :], xs[:, n, :], ACT.Relu, bias=ln_bias[:, s % 2:s % 2 + 1],
                                     scale=ln_scale[:, s % 2:s % 2 + 1]).then_inc(y_ok, 1)

            def after_quad(layer, R, first, q, tail=False):
                hooks = []
                for s in range(S):
                    hooks.append((28 + 2 * s, lambda l, r, s=s: evac(l, r, s)))
                    hooks.append((31 + 2 * s, lambda l, r, s=s: copy_T(l, r, s)))
                    hooks.append((38 + 2 * s, lambda l, r, s=s: make_y(r, s) if l == 0 else None))
                for at, f in sorted(hooks, key=lambda z: z[0]):
                    if not tail and at == q:
                        f(layer, R)
                    if at == q + QUADS and not (layer == 0 and first):
                        if tail:
                            f(layer, R)
                        elif first:
                            f(layer - 1, MR - 1)
                        else:
                            f(layer, R - 1)

            def layer_hi(layer):
                def body(R, first, last):
                    for q in range(QUADS):
                        n = (layer * MR + R) * QUADS + q
                        act.wait_ge(quad_T, n + 1)
                        if not (isinstance(n, int) and n < RING):
                            act.wait_ge(quad_M, n - RING + 1)
                        nc.scalar.activation(hi[:, q % RING, :], tbank(q), ACT.Copy).then_inc(hi_ok, 1)
                        after_quad(layer, R, first, q)
                return body

            macro_rows(act, layer_hi(0), True, False)
            macro_rows(act, layer_hi(1), True, False)
            for q in range(QUADS):
                after_quad(1, MR - 1, False, q, tail=True)

        @block.vector
        def _(dve):
            nc.vector.memset(ut[:, :, HID:HID + 1], 1.0).then_inc(dve_step, 1)
            nc.vector.memset(ut[:, :, HID + 1:UW], 0.0).then_inc(dve_step, 1)
            dve.wait_ge(dve_step, 2)
            dve.wait_ge(const_in, 96)
            dve.wait_ge(x_in, 16)
            base = 2
            PER_TILE = 4

            with dve.Fori(0, T // 2) as i:
                for k in range(2):
                    r = 2 * i + k
                    at = base + PER_TILE * r
                    nc.vector.bn_stats(stats[:, k, :], xs[:, r, :]).then_inc(dve_step, 1)
                    wait_apart(dve, dve_step, at + 1)
                    nc.vector.bn_aggr(mv[:, k, :], stats[:, k, :]).then_inc(stats_ok, 1)
                    dve.wait_ge(row_in[k], 16 * (i + 1))
                    nc.vector.tensor_reduce(sums[:, k, 1:2],
                                            strips[:, 4 * k + 2:4 * k + 4, :].rearrange("p a n -> p (a n)"),
                                            AX.X, ALU.add).then_inc(sum_dve, 1)
                    dve.wait_ge(u_ps, r + 1)
                    nc.vector.tensor_tensor(ut[:, k, 0:HID], ps[:, 2 + k, 0:HID], b1_all[:, :], ALU.add
                                            ).then_inc(dve_step, 1)
                    dve.wait_ge(dve_step, at + 2)
                    dve.wait_ge(deg_ok, r + 1)
                    nc.vector.tensor_scalar(us[:, k, :], ut[:, k, :], d1[:, bass.ds(r, 1)], None, ALU.mult
                                            ).then_inc(dve_step, 1)
                    dve.wait_ge(dve_step, at + 3)
                    nc.vector.tensor_copy(U[:, r, 0, :], us[:, k, :]).then_inc(dve_step, 1)
                    dve.wait_ge(dve_step, at + 4)
                    nc.vector.tensor_tensor(U[:, r, 1, :], us[:, k, :], U[:, r, 0, :].bitcast(F32),
                                            ALU.subtract).then_inc(U_ok, 1)
            base += PER_TILE * T

            L0_STEPS = 3
            L1_STEPS = 1

            def combine(layer, R, s):
                n = (layer * MR + R) * S + s
                w = DF if layer else UW
                deg = (d2 if layer else d1)[:, bass.ds(R * S + s, 1)]
                dve.wait_ge(accb_ok, n + 1)
                nc.vector.scalar_tensor_tensor(out=agg[:, s, 0:w], in0=acc(s)[:, 0:w], scalar=deg,
                                               in1=accb[:, s % 2, 0:w], op0=ALU.mult, op1=ALU.add
                                               ).then_inc(agg_ok, 1)

            def finish(layer, R, s):
                r = R * S + s
                n = (layer * MR + R) * S + s
                if layer == 0:
                    at = base + L0_STEPS * r
                    dve.wait_ge(agg_ok, n + 1)
                    nc.vector.scalar_tensor_tensor(out=xs[:, r, :], in0=b2_all[:, :],
                                                   scalar=agg[:, s, HID:HID + 1], in1=xs[:, r, :],
                                                   op0=ALU.mult, op1=ALU.add).then_inc(dve_step, 1)
                    dve.wait_ge(dve_step, at + 1)
                    dve.wait_ge(fin_ps, n + 1)
                    nc.vector.tensor_tensor(xs[:, r, :], xs[:, r, :], acc(s)[:, HID:HID + DF], ALU.add
                                            ).then_inc(fin_read, 1)
                    wait_apart(dve, fin_read, n + 1)
                    nc.vector.bn_stats(stats[:, s % 2, :], xs[:, r, :]).then_inc(dve_step, 1)
                    dve.wait_ge(dve_step, at + 2)
                    wait_apart(dve, ln_ok, T + r - 1)
                    nc.vector.bn_aggr(mv[:, s % 2, :], stats[:, s % 2, :]).then_inc(stats_ok, 1)
                    nc.vector.sem_inc(dve_step, 1)
                else:
                    at = base + L0_STEPS * T + L1_STEPS * r
                    dve.wait_ge(fin_ps, n + 1)
                    if not (isinstance(R, int) and R == 0):
                        dve.wait_ge(out_st[s], 16 * R)
                    nc.vector.tensor_tensor(ot[:, s, :], acc(s)[:, DF:2 * DF], b_all[:, :], ALU.add
                                            ).then_inc(fin_read, 1)
                    dve.wait_ge(fin_read, n + 1)
                    nc.vector.scalar_tensor_tensor(out=ot[:, s, :], in0=ot[:, s, :], scalar=0.0,
                                                   in1=xs[:, r, :], op0=ALU.max, op1=ALU.add
                                                   ).then_inc(out_ok, 1)

            def after_quad(layer, R, first, q, tail=False):
                hooks = []
                for s in range(S):
                    hooks.append((28 + 2 * s, lambda l, r, s=s: combine(l, r, s)))
                    hooks.append((34 + 2 * s, lambda l, r, s=s: finish(l, r, s)))
                for at, f in sorted(hooks, key=lambda z: z[0]):
                    if not tail and at == q:
                        f(layer, R)
                    if at == q + QUADS and not (layer == 0 and first):
                        if tail:
                            f(layer, R)
                        elif first:
                            f(layer - 1, MR - 1)
                        else:
                            f(layer, R - 1)

            def layer_lo(layer):
                def body(R, first, last):
                    for q in range(QUADS):
                        n = (layer * MR + R) * QUADS + q
                        dve.wait_ge(hi_ok, n + 1)
                        nc.vector.tensor_tensor(lo[:, q % RING, :], tbank(q), hi[:, q % RING, :].bitcast(F32),
                                                ALU.subtract).then_inc(lo_ok, 1)
                        after_quad(layer, R, first, q)
                return body

            macro_rows(dve, layer_lo(0), True, False)
            macro_rows(dve, layer_lo(1), True, False)
            for q in range(QUADS):
                after_quad(1, MR - 1, False, q, tail=True)

        @block.tensor
        def _(pe):
            pe.wait_ge(ident_ok, 1)
            pe.wait_ge(ident_r_ok, 1)
            pe.wait_ge(const_in, 96)
            for k in range(KF):
                nc.tensor.transpose(ps[:, 0, k * P:(k + 1) * P], w_in[:, 0, k * P:(k + 1) * P], ident[:, :])
                last = nc.tensor.transpose(ps[:, 1, k * P:(k + 1) * P], w_in[:, 1, k * P:(k + 1) * P],
                                           ident[:, :])
            last.then_inc(wT_ps, 1)
            pe.wait_ge(wT_ok, 1)

            with pe.Fori(0, T // 2) as i:
                for k in range(2):
                    r = 2 * i + k
                    pe.wait_ge(h_ok, r + 1)
                    for f in range(KF):
                        last = nc.tensor.transpose(ps[:, k, f * P:(f + 1) * P], h[:, k, f * P:(f + 1) * P],
                                                   ident[:, :])
                    last.then_inc(hT_ps, 1)
                    pe.wait_ge(hT_ok, r + 1)
                    for f in range(KF):
                        last = nc.tensor.matmul(ps[:, 2 + k, 0:HID], hT[:, k, f * P:(f + 1) * P],
                                                W1T[:, f, :], start=f == 0, stop=f == KF - 1)
                    last.then_inc(u_ps, 1)

            def transpose_quad(layer, R, q):
                n = (layer * MR + R) * QUADS + q
                over, q = divmod(q, QUADS)
                g, part = divmod(q, QS)
                slot = g % SLOTS
                if part == 0:
                    uses = (layer * MR + R + over) * (STR // SLOTS) + g // SLOTS
                    pe.wait_ge(strip_in[slot], 16 * (uses + 1))
                if not (isinstance(n, int) and n < RING):
                    pe.wait_ge(lo_ok, n - RING + 1)
                for j in range(JQ):
                    last = nc.tensor.transpose(tbank(q)[:, j * P:(j + 1) * P],
                                               strips[:, slot, part * QW + j * P:part * QW + (j + 1) * P],
                                               ident[:, :])
                last.then_inc(quad_T, 1)

            def multiply_quad(layer, R, q):
                n = (layer * MR + R) * QUADS + q
                g, part = divmod(q, QS)
                c, s = divmod(g, S)
                w = DF if layer else UW
                right = Y if layer else U
                opens = c == 0 and part == 0
                closes = c == PC - 1 and part == QS - 1
                if opens:
                    m = (layer * MR + R) * S + s
                    if isinstance(m, int) and m < S:
                        pe.wait_ge(U_ok, T)
                    else:
                        pe.wait_ge(fin_read, m - S + 1)
                    if layer == 0:
                        nc.tensor.matmul(acc(s)[:, 0:2 * w], ident_r[:, :],
                                         U[:, R * S + s, :, :].rearrange("p a n -> p (a n)"),
                                         start=True, stop=False)
                if layer == 1 and isinstance(R, int) and R == 0:
                    pe.wait_ge(Y_ok, FREE_Y + (c * SW + (part + 1) * QW) // P)
                pe.wait_ge(lo_ok, n + 1)
                for j in range(JQ):
                    t = (c * SW + part * QW) // P + j
                    both = right[:, t, :, :].rearrange("p a n -> p (a n)")
                    nc.tensor.matmul(acc(s)[:, 0:2 * w], hi[:, q % RING, j * P:(j + 1) * P], both,
                                     start=opens and j == 0 and layer == 1, stop=False)
                    last = nc.tensor.matmul(acc(s)[:, 0:w], lo[:, q % RING, j * P:(j + 1) * P],
                                            right[:, t, 0, :], start=False, stop=closes and j == JQ - 1)
                last.then_inc(quad_M, 1)

            def transpose_agg(layer, R, s):
                n = (layer * MR + R) * S + s
                pe.wait_ge(agg_ok, n + 1)
                for f in range((DF if layer else HID) // P):
                    last = nc.tensor.transpose(acc(s)[:, f * P:(f + 1) * P], agg[:, s, f * P:(f + 1) * P],
                                               ident[:, :])
                last.then_inc(agg_ps, 1)

            def project(layer, R, s):
                n = (layer * MR + R) * S + s
                pe.wait_ge(aggT_ok, n + 1)
                if layer == 0:
                    nc.tensor.matmul(acc(s)[:, HID:HID + DF], aggT[:, s % 2, 0:HID], W2T[:, :],
                                     start=True, stop=True).then_inc(fin_ps, 1)
                else:
                    for f in range(KF):
                        last = nc.tensor.matmul(acc(s)[:, DF:2 * DF], aggT[:, s % 2, f * P:(f + 1) * P],
                                                Wm[:, f, :], start=f == 0, stop=f == KF - 1)
                    last.then_inc(fin_ps, 1)

            def after_strip(layer, R, first, g, tail=False):
                hooks = []
                for s in range(S):
                    hooks.append((STR - 3 + s, lambda l, r, s=s: transpose_agg(l, r, s)))
                    hooks.append((STR - 2 + s, lambda l, r, s=s: project(l, r, s)))
                for at, f in sorted(hooks, key=lambda z: z[0]):
                    if not tail and at == g:
                        f(layer, R)
                    if at == g + STR and not (layer == 0 and first):
                        if tail:
                            f(layer, R)
                        elif first:
                            f(layer - 1, MR - 1)
                        else:
                            f(layer, R - 1)

            def layer_products(layer):
                def body(R, first, last):
                    if layer == 0 and first:
                        for q in range(AHEAD):
                            transpose_quad(layer, R, q)
                    for q in range(QUADS):
                        if not (last and q + AHEAD >= QUADS):
                            transpose_quad(layer, R, q + AHEAD)
                        multiply_quad(layer, R, q)
                        if q % QS == QS - 1:
                            after_strip(layer, R, first, q // QS)
                return body

            macro_rows(pe, layer_products(0), True, False)
            macro_rows(pe, layer_products(1), True, True)
            for g in range(STR):
                after_strip(1, MR - 1, False, g, tail=True)


_INS = ['x', 'adj', 'L0_gnn_W1', 'L0_gnn_b1', 'L0_gnn_W2', 'L0_gnn_b2', 'L1_gnn_W', 'L1_gnn_b']


def kernel(**inputs):
    import numpy as _np
    import concourse.bacc as _bacc
    from concourse import mybir as _mybir
    from concourse.bass_utils import run_bass_kernel_spmd as _run

    nc = _bacc.Bacc("TRN2", target_bir_lowering=False, num_devices=1)
    arrays, args = {}, []
    for name in _INS:
        a = _np.ascontiguousarray(inputs[name])
        arrays[f"in_{name}_dram"] = a
        args.append(nc.dram_tensor(f"in_{name}_dram", a.shape, _mybir.dt.from_np(a.dtype), kind="ExternalInput").ap())
    o = nc.dram_tensor("out_0_dram", inputs['x'].shape, _mybir.dt.float32, kind="ExternalOutput").ap()
    gnn_kernel(nc, *args, o)
    r = _run(nc, [arrays], core_ids=[0])
    return r.results[0]["out_0_dram"]
```

```python
from contextlib import ExitStack

import concourse.bass as bass
from concourse import mybir

P = 128
BL = 32
F32 = mybir.dt.float32
F32R = mybir.dt.float32r
ALU = mybir.AluOpType
ACT = mybir.ActivationFunctionType
AX = mybir.AxisListType
LN_EPS = 1e-5
TINY = 1e-30


def is_first(i):
    return isinstance(i, int) and i == 0


def segment(eng, trips, peel, body):
    for i in range(peel):
        body(i)
    with eng.Fori(int(peel), trips) as i:
        body(i)


def gnn_kernel(nc, x, adj, W1, b1, W2, b2, W, b, out):
    N, DF = x.shape
    HID = W1.shape[0]
    T = N // P
    KF = DF // P
    G = P // BL
    NG = N // G
    QT = 4
    QW = QT * P
    QC = QT * BL
    NQ = T // QT
    SR = 8
    SQ = SR // QT
    NB = T // SR
    RING = 4
    U4 = 4
    U2 = 2
    UW = HID + 2
    AHEAD = 3
    MINE = RING - 1

    q1 = [SR * SQ * B * (B - 1) // 2 for B in range(NB + 1)]
    P0 = T - SR

    STEPS = ("evac", "combine", "turn", "copy", "project", "finish", "norm", "y", "split")
    LAGS = {(2, 2): (1, 2, 3, 4, 4, 6, 6, 8, 8),
            (2, 4): (4, 4, 5, 8, 8, 10, 10, 13, 14),
            (2, 6): (4, 5, 5, 9, 9, 11, 11, 14, 15),
            (2, 8): (4, 5, 5, 9, 9, 11, 11, 14, 15),
            3: (4, 5, 5, 9, 9, 12, 12, 14, 14)}
    SOON = {4: (1, 1, 2, 2, 2, 2, 2, 3, 3),
            6: (4, 4, 4, 4, 4, 4, 4, 5, 5),
            8: (3, 3, 3, 5, 5, 5, 5, 7, 7)}
    BACK = 4
    PASS1 = {0: (3, 3, 0, 0, 0, 0), 2: (1, 3, 0, 1, 1, 1), 4: (2, 3, 1, 2, 3, 0), 6: (1, 3, 0, 3, 4, 2)}
    def quads_of(pas, B):
        if pas == 2:
            return list(range(SQ * B, SQ * (B + 1))) + list(reversed(range(SQ * (B + 1), NQ)))
        return list(reversed(range(SQ * (B + 1))))

    class Row:

        def __init__(self, seg, i, k):
            self.seg = seg
            per = len(seg.supers)
            own = seg.supers[k % per]
            self.pas = seg.pas
            self.own = own
            self.quads = quads_of(seg.pas, own)
            self.n = seg.row0 + seg.U * i + k
            self.m = self.n - (seg.pas - 2) * T
            self.r = i * -(seg.U // per) + (SR * own + SR - 1 - k // per)
            self.slot = k % 2
            self.K = len(self.quads)
            self.before = seg.before(k)
            self.step_quads = seg.before(seg.U)
            self.q0 = seg.quad0 + self.step_quads * i + self.before
            self.turn0 = i * (self.step_quads // RING) + seg.quad0 // RING
            self.layer0 = seg.pas == 2
            self.layer1 = seg.pas == 3 or own < NB - 1
            self.part = own > 0 if seg.pas == 2 else own < NB - 1
            self.parts = seg.parts[self.slot] + seg.U // 2 * i + k // 2 + 1

        def ring(self, q):
            return self.turn0 + (self.before + q) // RING, (self.before + q) % RING

    class Segment:

        def __init__(self, pas, supers, U, last):
            self.pas, self.supers, self.U, self.last = pas, supers, U, last
            self.rows = SR * len(supers)
            self.trips = self.rows // U
            self.row0 = last.row0 + last.rows if last else 0
            self.quad0 = last.quad0 + last.trips * last.before(last.U) if last else q1[NB]
            self.parts = [0, 0]
            if last and last.pas == pas:
                self.parts = [last.parts[k] + (last.rows // 2 if last.supers[k % len(last.supers)] < NB - 1 else 0)
                              for k in range(2)]

        def before(self, k):
            return sum(len(quads_of(self.pas, self.supers[j % len(self.supers)])) for j in range(k))

        def row(self, i, k):
            if 0 <= k < self.U:
                return Row(self, i, k)
            if not isinstance(i, int) or i + k // self.U >= 0:
                return Row(self, i + k // self.U, k % self.U)
            return Row(self.last, *divmod(self.last.rows + self.U * i + k, self.last.U)) if self.last else None

        def due(self, i, k, q):
            serial = self.pas == 2 or self.last.pas == 2
            for d in reversed(range(1, BACK + 1)):
                row = self.row(i, k - d)
                if not row or serial and row.seg is not self and not (is_first(i) and k == 0):
                    continue
                since = sum(self.row(i, j).K for j in range(k - d + 1, k))
                lags = LAGS[3 if row.pas == 3 else (2, row.K)]
                for j, (step, lag) in enumerate(zip(STEPS, lags)):
                    if j < 2 and k - d + 1 < self.U:
                        lag = min(lag, self.row(i, k - d + 1).K)
                    if serial and row.seg is not self:
                        if lag <= since:
                            continue
                        soon = SOON[self.row(i, k).K][j] - (d - 1)
                        lag = max(min(lag, since + soon), since + 1)
                    if lag == since + q + 1:
                        yield step, row

    segments = []
    for pas, supers in ((2, (3,)), (2, (2,)), (2, (1,)), (2, (0,)), (3, (3, 0)), (3, (2, 1))):
        segments.append(Segment(pas, supers, 2 * len(supers), segments[-1] if segments else None))
    end = segments[-1]

    def last_steps():
        for q in range(max(LAGS[3])):
            yield from end.due(end.trips - 1, end.U, q)

    with ExitStack() as ctx:
        def sb(name, shape, dt=F32):
            return ctx.enter_context(nc.sbuf_tensor(name, shape, dt))

        def sem(name):
            return ctx.enter_context(nc.semaphore(name))

        with ExitStack() as early_ctx:
            rows = early_ctx.enter_context(nc.sbuf_tensor("rows", [P, U4, N], F32))
        strips = sb("strips", [P, U2, N])
        Y = sb("Y", [P, T, 2, DF], F32R)
        xs = sb("xs", [P, T, DF])
        U = sb("U", [P, T, 2, UW], F32R)
        part0 = sb("part0", [P, P0, UW])
        tq = sb("tq", [P, RING, QW])
        hi = sb("hi", [P, RING, QW], F32R)
        lo = sb("lo", [P, RING, QW], F32R)
        ident = sb("ident", [P, P])
        ident_r = sb("ident_r", [P, P], F32R)
        W1T = sb("W1T", [P, KF, HID])
        W2T = sb("W2T", [P, DF])
        Wm = sb("Wm", [P, KF, DF])
        b1_all = sb("b1_all", [P, HID])
        b2_all = sb("b2_all", [P, DF])
        b_all = sb("b_all", [P, DF])
        d1 = sb("d1", [P, T])
        d2 = sb("d2", [P, T])
        expo = sb("expo", [P, T])
        sums = sb("sums", [P, U4, G])
        pick = sb("pick", [P, (2 * G - 1) * BL])
        rowsum = sb("rowsum", [P, U2])
        stats = sb("stats", [P, 2, 6])
        mv = sb("mv", [P, 2, 2])
        stats_x = sb("stats_x", [P, T, 6])
        mv_x = sb("mv_x", [P, T, 2])
        ln_x = sb("ln_x", [P, 4, T])
        deg = sb("deg", [P, 4])
        mask = sb("mask", [P, 4])
        rstd = sb("rstd", [P, 4])
        ln_scale = sb("ln_scale", [P, 2])
        ln_bias = sb("ln_bias", [P, 2])
        h = sb("h", [P, 2, DF])
        colT = sb("colT", [P, 2, DF])
        w_in = colT
        ut = sb("ut", [P, 2, HID + 1])
        us = sb("us", [P, 2, UW])
        accb0 = sb("accb0", [P, 2, UW])
        accb1 = sb("accb1", [P, 2, DF])
        agg = sb("agg", [P, 2, DF])
        stage = sb("stage", [P, 2, DF])
        part1 = sb("part1", [P, 2, DF])
        spill = nc.dram_tensor("spill", (P0, P, DF), F32).ap()

        ps = ctx.enter_context(nc.psum_tensor("ps", [P, 8, 512], F32))

        def acc0(k):
            return ps[:, k, :]

        def acc1(k):
            return ps[:, 2 + k, :]

        def acc_sum(k):
            return acc0(k)[:, HID + 1:HID + 2]

        def fin(k):
            return ps[:, 4 + k, :]

        const_in = sem("const_in")
        x_in = sem("x_in")
        ident_ok = sem("ident_ok")
        ident_r_ok = sem("ident_r_ok")
        wT_ps = sem("wT_ps")
        wT_ok = sem("wT_ok")
        row_in = [sem(f"row_in{i}") for i in range(U4)]
        strip_in = [sem(f"strip_in{i}") for i in range(U2)]
        pick_ok = sem("pick_ok")
        sum_act = sem("sum_act")
        sum_ps = sem("sum_ps")
        sum_ok = sem("sum_ok")
        stats_ok = sem("stats_ok")
        ln_ok = sem("ln_ok")
        h_ok = sem("h_ok")
        hT_ps = sem("hT_ps")
        hT_ok = sem("hT_ok")
        u_ps = sem("u_ps")
        u_read = sem("u_read")
        deg_ok = sem("deg_ok")
        U_ok = sem("U_ok")
        quad_T = sem("quad_T")
        row_T = sem("row_T")
        hi_ok = sem("hi_ok")
        lo_ok = sem("lo_ok")
        lo_pool = sem("lo_pool")
        quad_M = sem("quad_M")
        accb0_ok = sem("accb0_ok")
        accb1_ok = sem("accb1_ok")
        comb0 = sem("comb0")
        comb1 = sem("comb1")
        agg_ok = sem("agg_ok")
        agg_ps = sem("agg_ps")
        aggT_ok = sem("aggT_ok")
        fin_ps = sem("fin_ps")
        fin_read = sem("fin_read")
        Y_ok = sem("Y_ok")
        stage_ok = sem("stage_ok")
        stage_st = [sem(f"stage_st{i}") for i in range(2)]
        part1_in = [sem(f"part1_in{i}") for i in range(2)]
        dve_step = sem("dve_step")
        x_b2 = sem("x_b2")
        x1_stats = sem("x1_stats")
        pool_step = sem("pool_step")
        waited = sem("waited")

        block = ctx.enter_context(nc.Block())

        def wait_apart(eng, s, n):
            eng.wait_ge(s, n)
            eng.sem_inc(waited, 1)

        adj_blocks = adj.rearrange("(g t k) (h c) -> t g h k c", g=G, k=BL, h=G)
        out_rows = out.rearrange("(g t k) f -> t g k f", g=G, k=BL)

        def ring1(B, i, s, q):
            K = SQ * B
            return i * (U4 * K // RING) + (q1[B] // RING + (s * K + q) // RING), (s * K + q) % RING

        def run_passes(eng, passes):
            for seg in segments:
                segment(eng, seg.trips, 2 if seg.pas == 2 else 1, passes(seg))

        @block.sync
        def _(sp):
            sp.dma_start(w_in[:, 0, :], W1).then_inc(const_in, 16)
            sp.dma_start(w_in[:, 1, :].rearrange("p (k h) -> p k h", k=KF),
                         W2.rearrange("(k p) h -> p k h", p=P)).then_inc(const_in, 16)

            def load_row(r, s):
                for g in range(G):
                    sp.dma_start(rows[:, s, g * NG:(g + 1) * NG], adj_blocks[r, g]).then_inc(row_in[s], 16)

            x_groups = x.rearrange("(g t k) f -> g k t f", g=G, k=BL)
            for g in range(G):
                sp.dma_start(xs[g * BL:(g + 1) * BL, :, :], x_groups[g]).then_inc(x_in, 16)
            for dst, src, s in ((b1_all, b1, stage_st[0]), (b2_all, b2, stage_st[1]), (b_all, b, const_in)):
                sp.dma_start(dst[:, :], src.rearrange("(a n) -> a n", a=1).to_broadcast([P, src.shape[0]])
                             ).then_inc(s, 16)
            sp.dma_start(Wm[:, :, :], W.rearrange("(k p) f -> p k f", p=P)).then_inc(const_in, 16)

            for s in range(U4):
                load_row(s, s)

            def next_rows(transposed):
                def body(i):
                    for s in range(U4):
                        r = U4 * i + s
                        wait_apart(sp, sum_act, 1 + G * (r - U4 + 1))
                        if transposed:
                            wait_apart(sp, row_T, r - U4 - SR + 1)
                        load_row(r, s)
                return body

            with sp.Fori(1, 3) as i:
                next_rows(False)(i)
            with sp.Fori(3, T // U4) as i:
                next_rows(True)(i)

            def load_strip(row):
                a, z = (SQ * row.own * QC, NG) if row.pas == 2 else (0, SQ * (row.own + 1) * QC)
                for g in range(G):
                    sp.dma_start(strips[:, row.slot, g * NG + a:g * NG + z],
                                 adj_blocks[row.r, g][:, :, a:z]).then_inc(strip_in[row.slot], 16)

            def load_part1(row):
                wait_apart(sp, agg_ok, row.n - 1)
                sp.dma_start(part1[:, row.slot, :], spill[row.r]).then_inc(part1_in[row.slot], 16)

            def passes(seg):
                def body(i):
                    for k in range(seg.U):
                        row, last = seg.row(i, k), seg.row(i, k - 1)
                        if isinstance(row.n, int) and row.n < U2:
                            wait_apart(sp, sum_act, 1 + G * (T - U4 + k + 1))
                            wait_apart(sp, row_T, P0 - U4 + k + 1)
                        else:
                            wait_apart(sp, row_T, P0 + row.n - U2 + 1)
                        load_strip(row)
                        if last and last.pas == 3 and last.part:
                            load_part1(last)
                return body

            run_passes(sp, passes)
            load_part1(end.row(end.trips - 1, end.U - 1))
            for k in range(U2):
                sp.wait_ge(stage_st[k], 16 + 16 * (P0 + T) // 2)

        @block.gpsimd
        def _(pool):
            nc.gpsimd.memset(expo[:, :], -0.5)
            nc.gpsimd.memset(ident[:, :], 0.0).then_inc(pool_step, 1)
            pool.wait_ge(pool_step, 1)
            nc.gpsimd.affine_select(out=ident[:, :], in_=ident[:, :], compare_op=ALU.not_equal, fill=1.0,
                                    base=0, pattern=[[-1, P]], channel_multiplier=1).then_inc(ident_ok, 1)
            pool.wait_ge(ident_ok, 1)
            nc.gpsimd.tensor_copy(ident_r[:, :], ident[:, :]).then_inc(ident_r_ok, 1)
            pool.sem_inc(Y_ok, 2)

            class Steps:

                def __init__(self, n):
                    self.n = n

                def __call__(self, ins):
                    ins.then_inc(pool_step, 1)
                    self.n = self.n + 1
                    wait_apart(pool, pool_step, self.n)

            step = Steps(1)
            pool.wait_ge(stats_ok, T)
            nc.gpsimd.tensor_scalar(ln_x[:, 2, :], mv_x[:, :, 0], -1.0, None, ALU.mult)
            step(nc.gpsimd.tensor_scalar(ln_x[:, 0, :], mv_x[:, :, 1], LN_EPS, None, ALU.add))
            step(nc.gpsimd.tensor_tensor(ln_x[:, 1, :], ln_x[:, 0, :], expo[:, :], ALU.pow))
            nc.gpsimd.tensor_tensor(ln_x[:, 3, :], ln_x[:, 2, :], ln_x[:, 1, :], ALU.mult).then_inc(ln_ok, 1)
            pool.wait_ge(ln_ok, 1)
            pool.sem_inc(ln_ok, 1)

            def lower(g, j):
                if j < MINE:
                    return
                pool.wait_ge(hi_ok, RING * g + j + 1)
                nc.gpsimd.tensor_tensor(lo[:, j, :], tq[:, j, :], hi[:, j, :].bitcast(F32), ALU.subtract
                                        ).then_inc(lo_pool, 1)

            def degrees(r, s):
                step = Steps(3 + STEPS1 * r)
                wait_apart(pool, sum_ok, r + 1)
                nc.gpsimd.tensor_copy(deg[:, 0:1], rowsum[:, s % 2:s % 2 + 1])
                step(nc.gpsimd.tensor_scalar(deg[:, 1:2], rowsum[:, s % 2:s % 2 + 1], 1.0, None, ALU.add))
                nc.gpsimd.tensor_scalar(mask[:, 0:2], deg[:, 0:2], 0.0, None, ALU.is_gt)
                step(nc.gpsimd.tensor_scalar(deg[:, 2:4], deg[:, 0:2], TINY, None, ALU.max))
                step(nc.gpsimd.tensor_tensor(mask[:, 2:4], deg[:, 2:4], expo[:, 0:2], ALU.pow))
                nc.gpsimd.tensor_tensor(d2[:, bass.ds(r, 1)], mask[:, 2:3], mask[:, 0:1], ALU.mult)
                nc.gpsimd.tensor_tensor(d1[:, bass.ds(r, 1)], mask[:, 3:4], mask[:, 1:2], ALU.mult
                                        ).then_inc(deg_ok, 1)

            STEPS1, STEPS2 = 3, 3

            def pass1(B):
                K = SQ * B

                def body(i):
                    for s in range(U4):
                        r = SR * B + U4 * i + s
                        for q in range(max(K, 1)):
                            if q == PASS1[K][5] and not (isinstance(r, int) and r == 0):
                                degrees(r - 1, s - 1)
                            if K:
                                lower(*ring1(B, i, s, q))
                return body

            for B in range(NB):
                segment(pool, SR // U4, B == 0, pass1(B))
            degrees(T - 1, U4 - 1)
            pool.wait_ge(deg_ok, T)

            def after(step_name, row):
                if row.pas == 3:
                    return
                k, m, r = row.slot, row.m, row.r
                if step_name == "norm":
                    step = Steps(3 + STEPS1 * T + STEPS2 * m)
                    wait_apart(pool, stats_ok, T + m + 1)
                    step(nc.gpsimd.tensor_scalar(rstd[:, 0:1], mv[:, k, 1:2], LN_EPS, None, ALU.add))
                    step(nc.gpsimd.tensor_tensor(rstd[:, 1:2], rstd[:, 0:1], expo[:, 0:1], ALU.pow))
                    step(nc.gpsimd.tensor_tensor(ln_scale[:, k:k + 1], rstd[:, 1:2], d2[:, bass.ds(r, 1)],
                                                 ALU.mult))
                    nc.gpsimd.tensor_scalar(ln_bias[:, k:k + 1], mv[:, k, 0:1], ln_scale[:, k:k + 1], -1.0,
                                            ALU.mult, ALU.mult).then_inc(ln_ok, 1)
                if step_name == "split":
                    wait_apart(pool, h_ok, T + m + 1)
                    nc.gpsimd.tensor_tensor(Y[:, r, 1, :], h[:, k, :], Y[:, r, 0, :].bitcast(F32),
                                            ALU.subtract).then_inc(Y_ok, 1)

            def passes(seg):
                def body(i):
                    for k in range(seg.U):
                        row = seg.row(i, k)
                        for q in range(row.K):
                            lower(*row.ring(q))
                            for step, earlier in seg.due(i, k, q):
                                after(step, earlier)
                return body

            run_passes(pool, passes)

        @block.scalar
        def _(act):
            act.sem_inc(sum_act, 1)
            act.wait_ge(wT_ps, 1)
            nc.scalar.activation(W1T[:, :, :].rearrange("p k h -> p (k h)"), ps[:, 0, 0:KF * HID], ACT.Copy)
            nc.scalar.activation(W2T[:, :], ps[:, 1, 0:DF], ACT.Copy).then_inc(wT_ok, 1)

            def upper(g, j):
                act.wait_ge(quad_T, RING * g + j + 1)
                act.wait_ge(quad_M, RING * g + j + 1)
                nc.scalar.activation(hi[:, j, :], tq[:, j, :], ACT.Copy).then_inc(hi_ok, 1)

            def evac0(e, r, k, done):
                act.wait_ge(quad_M, RING + done)
                act.wait_ge(comb0, e + 1)
                nc.scalar.activation(accb0[:, k, :], acc0(k)[:, UW:2 * UW], ACT.Copy,
                                     scale=d1[:, bass.ds(r, 1)]).then_inc(accb0_ok, 1)

            def evac1(f, r, k, done):
                act.wait_ge(quad_M, RING + done)
                act.wait_ge(comb1, f + 1)
                nc.scalar.activation(accb1[:, k, :], acc1(k)[:, DF:2 * DF], ACT.Copy,
                                     scale=d2[:, bass.ds(r, 1)]).then_inc(accb1_ok, 1)

            def pass1(B):
                K = SQ * B

                def body(i):
                    for s in range(U4):
                        r = SR * B + U4 * i + s
                        n0 = q1[B] + (U4 * i + s) * K
                        nc.scalar.activation(h[:, s % 2, :], xs[:, r, :], ACT.Relu,
                                             bias=ln_x[:, 3, bass.ds(r, 1)], scale=ln_x[:, 1, bass.ds(r, 1)]
                                             ).then_inc(h_ok, 1)
                        act.wait_ge(row_in[s], 16 * G * (SR // U4 * B + i + 1))
                        for q in range(max(K, G)):
                            if q < G:
                                act.wait_ge(sum_act, 1 + G * r + q)
                                nc.scalar.activation(
                                    ps[:, 4:6, :].rearrange("p a n -> p (a n)")[:, K * QC:NG],
                                    rows[:, s, q * NG + K * QC:(q + 1) * NG],
                                    ACT.Copy, accum_out=sums[:, s, q:q + 1]).then_inc(sum_act, 1)
                            if q < K:
                                upper(*ring1(B, i, s, q))
                            if q == PASS1[K][0]:
                                act.wait_ge(hT_ps, r + 1)
                                nc.scalar.activation(colT[:, s % 2, :], ps[:, 2 + s % 2, 0:DF], ACT.Copy
                                                     ).then_inc(hT_ok, 1)
                            if q == PASS1[K][1] and B and not (B == 1 and is_first(i) and s == 0):
                                act.wait_ge(deg_ok, r)
                                evac0(r - 1 - SR, r - 1, (s - 1) % 2, n0)
                return body

            act.wait_ge(ln_ok, 2)
            for B in range(NB):
                segment(act, SR // U4, B < 2, pass1(B))
            act.wait_ge(deg_ok, T)
            evac0(P0 - 1, T - 1, 1, q1[NB])

            def after(step, row):
                k, m, r = row.slot, row.m, row.r
                if step == "evac":
                    if row.layer0:
                        evac0(P0 + m, r, k, row.q0 + row.K)
                    if row.layer1:
                        evac1(m - SR if row.pas == 2 else P0 + m, r, k, row.q0 + row.K)
                if step == "copy":
                    w = HID if row.layer0 else DF
                    act.wait_ge(agg_ps, row.n + 1)
                    nc.scalar.activation(colT[:, k, 0:w], fin(k)[:, 0:w], ACT.Copy).then_inc(aggT_ok, 1)
                    if row.layer0 and row.layer1:
                        wait_apart(act, stage_ok, m - SR + 1)
                        act.dma_start(spill[r], stage[:, k, :]).then_inc(stage_st[k], 16)
                if step == "y" and row.pas == 2:
                    act.wait_ge(ln_ok, 2 + m + 1)
                    act.wait_ge(Y_ok, m + 1)
                    for dst in (h[:, k, :], Y[:, r, 0, :]):
                        last = nc.scalar.activation(dst, xs[:, r, :], ACT.Relu, bias=ln_bias[:, k:k + 1],
                                                    scale=ln_scale[:, k:k + 1])
                    last.then_inc(h_ok, 1)
                if step == "y" and row.pas == 3:
                    wait_apart(act, stage_ok, P0 + m + 1)
                    act.dma_start(out_rows[r], stage[:, k, :]).then_inc(stage_st[k], 16)

            def passes(seg):
                def body(i):
                    for k in range(seg.U):
                        row = seg.row(i, k)
                        for q in range(row.K):
                            upper(*row.ring(q))
                            for step, earlier in seg.due(i, k, q):
                                after(step, earlier)
                return body

            run_passes(act, passes)
            for step, row in last_steps():
                after(step, row)

        @block.vector
        def _(dve):
            nc.vector.memset(ut[:, :, HID:HID + 1], 1.0).then_inc(dve_step, 1)
            nc.vector.memset(us[:, :, HID + 1:UW], 1.0).then_inc(dve_step, 1)
            dve.wait_ge(dve_step, 2)
            for s, n in ((lo_ok, MINE), (lo_pool, 1), (comb0, 2), (comb1, 2), (u_read, 2), (fin_read, 2)):
                dve.sem_inc(s, n)
            nc.vector.memset(pick[:, :], 0.0).then_inc(dve_step, 1)
            dve.wait_ge(dve_step, 3)
            dve.wait_ge(ident_ok, 1)
            nc.vector.tensor_reduce(pick[:, (G - 1) * BL:G * BL], ident[:, :].rearrange("p (h k) -> p k h", h=G),
                                    AX.X, ALU.add).then_inc(pick_ok, 1)
            dve.wait_ge(const_in, 64)
            dve.wait_ge(stage_st[0], 16)
            dve.wait_ge(stage_st[1], 16)
            dve.wait_ge(x_in, 16 * G)
            for t in range(T):
                nc.vector.bn_stats(stats_x[:, t, :], xs[:, t, :]).then_inc(dve_step, 1)
            dve.wait_ge(dve_step, 3 + T)
            for t in range(T):
                nc.vector.bn_aggr(mv_x[:, t, :], stats_x[:, t, :]).then_inc(stats_ok, 1)
            STEPS1 = 2
            base1 = 3 + T

            def turn(g, j, src, c):
                if j < MINE:
                    dve.wait_ge(lo_ok, MINE * g + j + 1)
                else:
                    dve.wait_ge(lo_pool, g + 1)
                blocks = src.rearrange("p (g t c) -> p g t c", g=G, c=BL)
                dst = tq[:, j, :].rearrange("p (t g c) -> p g t c", t=QT, g=G)
                nc.vector.transpose(dst, blocks[:, :, c * QT:(c + 1) * QT, :]).then_inc(quad_T, 1)

            def row_free(n):
                dve.wait_ge(quad_T, n)
                dve.sem_inc(row_T, 1)

            def lower(g, j):
                if j >= MINE:
                    return
                dve.wait_ge(hi_ok, RING * g + j + 1)
                nc.vector.tensor_tensor(lo[:, j, :], tq[:, j, :], hi[:, j, :].bitcast(F32),
                                        ALU.subtract).then_inc(lo_ok, 1)

            def combine0(e, r, k, dst):
                dve.wait_ge(accb0_ok, e + 1)
                nc.vector.scalar_tensor_tensor(out=dst, in0=acc0(k)[:, 0:UW], scalar=d1[:, bass.ds(r, 1)],
                                               in1=accb0[:, k, :], op0=ALU.mult, op1=ALU.add
                                               ).then_inc(comb0, 1)

            def combine1(f, r, k, dst):
                dve.wait_ge(accb1_ok, f + 1)
                nc.vector.scalar_tensor_tensor(out=dst, in0=acc1(k)[:, 0:DF], scalar=d2[:, bass.ds(r, 1)],
                                               in1=accb1[:, k, :], op0=ALU.mult, op1=ALU.add
                                               ).then_inc(comb1, 1)

            def make_U(r, k):
                at = base1 + STEPS1 * r
                dve.wait_ge(u_ps, r + 1)
                nc.vector.tensor_tensor(ut[:, k, 0:HID], ps[:, 2 + k, DF:DF + HID], b1_all[:, :], ALU.add
                                        ).then_inc(u_read, 1)
                dve.wait_ge(u_read, 2 + r + 1)
                dve.wait_ge(deg_ok, r + 1)
                nc.vector.tensor_scalar(us[:, k, 0:HID + 1], ut[:, k, :], d1[:, bass.ds(r, 1)], None, ALU.mult
                                        ).then_inc(dve_step, 1)
                dve.wait_ge(dve_step, at + 1)
                nc.vector.tensor_copy(U[:, r, 0, :], us[:, k, :]).then_inc(dve_step, 1)
                dve.wait_ge(dve_step, at + 2)
                nc.vector.tensor_tensor(U[:, r, 1, :], us[:, k, :], U[:, r, 0, :].bitcast(F32),
                                        ALU.subtract).then_inc(U_ok, 1)

            def pass1(B):
                K = SQ * B

                def body(i):
                    for s in range(U4):
                        r = SR * B + U4 * i + s
                        n0 = q1[B] + (U4 * i + s) * K
                        def quad(q):
                            return ring1(B, i, s, q)

                        if K:
                            dve.wait_ge(row_in[s], 16 * G * (SR // U4 * B + i + 1))
                        for q in range(min(AHEAD, K)):
                            turn(*quad(q), rows[:, s, :], q)
                        last = max(K, 1) - 1
                        first = isinstance(r, int) and r == 0
                        for q in range(last + 1):
                            if K:
                                lower(*quad(q))
                            if q + AHEAD < K:
                                turn(*quad(q + AHEAD), rows[:, s, :], q + AHEAD)
                            if q == K - 1:
                                row_free(n0 + K)
                            if q == PASS1[K][2] and not first:
                                row_sum(r - 1, s - 1)
                            if q == PASS1[K][3] and not first:
                                make_U(r - 1, (s - 1) % 2)
                            if q == PASS1[K][4] and B and not (B == 1 and is_first(i) and s == 0):
                                combine0(r - 1 - SR, r - 1, (s - 1) % 2, part0[:, r - 1 - SR, :])
                return body

            def row_sum(r, s):
                dve.wait_ge(sum_ps, r + 1)
                nc.vector.tensor_copy(rowsum[:, s % 2:s % 2 + 1], acc_sum(s % 2)).then_inc(sum_ok, 1)

            for B in range(NB):
                segment(dve, SR // U4, B < 2, pass1(B))
            row_sum(T - 1, 1)
            make_U(T - 1, 1)
            combine0(P0 - 1, T - 1, 1, part0[:, P0 - 1, :])

            def after(step, row):
                k, m, r = row.slot, row.m, row.r
                if step == "combine" and row.pas == 2:
                    combine0(P0 + m, r, k, us[:, k, :] if row.part else agg[:, k, 0:UW])
                    dve.wait_ge(comb0, 2 + P0 + m + 1)
                    if row.part:
                        nc.vector.tensor_tensor(agg[:, k, 0:UW], us[:, k, :], part0[:, r - SR, :], ALU.add
                                                ).then_inc(agg_ok, 1)
                    else:
                        dve.sem_inc(agg_ok, 1)
                    if row.layer1:
                        wait_stage(m - SR, k)
                        combine1(m - SR, r, k, stage[:, k, :])
                        dve.wait_ge(comb1, 2 + m - SR + 1)
                        dve.sem_inc(stage_ok, 1)
                    dve.wait_ge(agg_ok, row.n + 1)
                    nc.vector.scalar_tensor_tensor(out=xs[:, r, :], in0=b2_all[:, :],
                                                   scalar=agg[:, k, HID:HID + 1], in1=xs[:, r, :],
                                                   op0=ALU.mult, op1=ALU.add).then_inc(x_b2, 1)
                if step == "combine" and row.pas == 3:
                    combine1(P0 + m, r, k, h[:, k, :] if row.part else agg[:, k, :])
                    dve.wait_ge(comb1, 2 + P0 + m + 1)
                    if row.part:
                        dve.wait_ge(part1_in[k], 16 * row.parts)
                        nc.vector.tensor_tensor(agg[:, k, :], h[:, k, :], part1[:, k, :], ALU.add
                                                ).then_inc(agg_ok, 1)
                    else:
                        dve.sem_inc(agg_ok, 1)
                if step == "finish":
                    if row.pas == 2:
                        dve.wait_ge(x_b2, m + 1)
                    dve.wait_ge(fin_ps, row.n + 1)
                    if row.pas == 2:
                        nc.vector.tensor_tensor(xs[:, r, :], xs[:, r, :], fin(k)[:, DF:2 * DF], ALU.add
                                                ).then_inc(fin_read, 1)
                        wait_apart(dve, fin_read, 2 + row.n + 1)
                        nc.vector.bn_stats(stats[:, k, :], xs[:, r, :]).then_inc(x1_stats, 1)
                        dve.wait_ge(x1_stats, m + 1)
                        wait_apart(dve, ln_ok, 2 + m - 1)
                        nc.vector.bn_aggr(mv[:, k, :], stats[:, k, :]).then_inc(stats_ok, 1)
                    else:
                        wait_stage(P0 + m, k)
                        nc.vector.tensor_tensor(stage[:, k, :], fin(k)[:, DF:2 * DF], b_all[:, :], ALU.add
                                                ).then_inc(fin_read, 1)
                        dve.wait_ge(fin_read, 2 + row.n + 1)
                        nc.vector.scalar_tensor_tensor(out=stage[:, k, :], in0=stage[:, k, :], scalar=0.0,
                                                       in1=xs[:, r, :], op0=ALU.max, op1=ALU.add
                                                       ).then_inc(stage_ok, 1)

            def wait_stage(f, k):
                dve.wait_ge(stage_st[k], 8 * (f - k) + 16)

            def passes(seg):
                def body(i):
                    for k in range(seg.U):
                        row = seg.row(i, k)
                        source = strips[:, row.slot, :]
                        dve.wait_ge(strip_in[row.slot], (row.n - row.slot) * (8 * G) + 16 * G)
                        for q in range(min(AHEAD, row.K)):
                            turn(*row.ring(q), source, row.quads[q])
                        for q in range(row.K):
                            lower(*row.ring(q))
                            if q + AHEAD < row.K:
                                turn(*row.ring(q + AHEAD), source, row.quads[q + AHEAD])
                            if q == row.K - 1:
                                row_free(row.q0 + row.K)
                            for step, earlier in seg.due(i, k, q):
                                after(step, earlier)
                return body

            run_passes(dve, passes)
            for step, row in last_steps():
                after(step, row)

        @block.tensor
        def _(pe):
            pe.sem_inc(quad_M, RING)
            pe.wait_ge(ident_ok, 1)
            pe.wait_ge(ident_r_ok, 1)
            pe.wait_ge(pick_ok, 1)
            pe.wait_ge(const_in, 64)
            for f in range(KF):
                nc.tensor.transpose(ps[:, 0, f * P:(f + 1) * P], w_in[:, 0, f * P:(f + 1) * P], ident[:, :])
                last = nc.tensor.transpose(ps[:, 1, f * P:(f + 1) * P], w_in[:, 1, f * P:(f + 1) * P],
                                           ident[:, :])
            last.then_inc(wT_ps, 1)
            pe.wait_ge(wT_ok, 1)

            def multiply(g, slot, c, layers, opens, closes, k, wait_Y=None, wait_U=None):
                if slot < MINE:
                    pe.wait_ge(lo_ok, MINE + MINE * g + slot + 1)
                else:
                    pe.wait_ge(lo_pool, 1 + g + 1)
                if wait_Y is not None:
                    pe.wait_ge(Y_ok, 2 + wait_Y)
                if wait_U is not None:
                    pe.wait_ge(U_ok, wait_U)
                for j in range(QT):
                    t = c * QT + j
                    a_hi = hi[:, slot, j * P:(j + 1) * P]
                    a_lo = lo[:, slot, j * P:(j + 1) * P]
                    for layer in layers:
                        right, w, a = (U, UW, acc0(k)) if layer == 0 else (Y, DF, acc1(k))
                        last = nc.tensor.matmul(a[:, 0:2 * w], a_hi,
                                                right[:, t, :, :].rearrange("p a n -> p (a n)"),
                                                start=opens[layer] and j == 0, stop=False)
                    for layer in layers:
                        right, w, a = (U, UW, acc0(k)) if layer == 0 else (Y, DF, acc1(k))
                        last = nc.tensor.matmul(a[:, 0:w], a_lo, right[:, t, 0, :], start=False,
                                                stop=closes and j == QT - 1)
                last.then_inc(quad_M, 1)

            def pass1(B):
                K = SQ * B

                def body(i):
                    for s in range(U4):
                        r = SR * B + U4 * i + s
                        if not (isinstance(r, int) and r == 0):
                            before(r - 1, s - 1, opens=B == 0 or B == 1 and is_first(i) and s == 0)
                        pe.wait_ge(h_ok, r + 1)
                        pe.wait_ge(u_read, r + 1)
                        for f in range(KF):
                            last = nc.tensor.transpose(ps[:, 2 + s % 2, f * P:(f + 1) * P],
                                                       h[:, s % 2, f * P:(f + 1) * P], ident[:, :])
                        last.then_inc(hT_ps, 1)
                        for q in range(K):
                            if q == 0:
                                pe.wait_ge(comb0, r - SR + 1)
                            multiply(*ring1(B, i, s, q), q, (0,), {0: q == 0}, False,
                                     s % 2, wait_U=QT * (q + 1) if is_first(i) else None)
                return body

            def before(r, s, opens=False):
                pe.wait_ge(hT_ok, r + 1)
                for f in range(KF):
                    last = nc.tensor.matmul(ps[:, 2 + s % 2, DF:DF + HID], colT[:, s % 2, f * P:(f + 1) * P],
                                            W1T[:, f, :], start=f == 0, stop=f == KF - 1)
                last.then_inc(u_ps, 1)
                pe.wait_ge(sum_act, 1 + G * (r + 1))
                for g in range(G):
                    z = (G - 1 - g) * BL
                    last = nc.tensor.matmul(acc_sum(s % 2), pick[:, z:z + P], sums[:, s % U4, g:g + 1],
                                            start=opens and g == 0, stop=g == G - 1)
                last.then_inc(sum_ps, 1)

            for B in range(NB):
                segment(pe, SR // U4, True, pass1(B))
            before(T - 1, U4 - 1)
            pe.wait_ge(U_ok, T)

            def after(step, row):
                k = row.slot
                if step == "turn":
                    pe.wait_ge(agg_ok, row.n + 1)
                    pe.wait_ge(fin_read, row.n + 1)
                    for f in range((HID if row.layer0 else DF) // P):
                        last = nc.tensor.transpose(fin(k)[:, f * P:(f + 1) * P],
                                                   agg[:, k, f * P:(f + 1) * P], ident[:, :])
                    last.then_inc(agg_ps, 1)
                if step == "project":
                    pe.wait_ge(aggT_ok, row.n + 1)
                    if row.layer0:
                        last = nc.tensor.matmul(fin(k)[:, DF:2 * DF], colT[:, k, 0:HID], W2T[:, :],
                                                start=True, stop=True)
                    else:
                        for f in range(KF):
                            last = nc.tensor.matmul(fin(k)[:, DF:2 * DF], colT[:, k, f * P:(f + 1) * P],
                                                    Wm[:, f, :], start=f == 0, stop=f == KF - 1)
                    last.then_inc(fin_ps, 1)

            def passes(seg):
                def body(i):
                    for k in range(seg.U):
                        row = seg.row(i, k)
                        for q, c in enumerate(row.quads):
                            if row.layer0 and q == 0:
                                pe.wait_ge(comb0, P0 + row.m + 1)
                                nc.tensor.matmul(acc0(row.slot)[:, 0:2 * UW], ident_r[:, :],
                                                 U[:, row.r, :, :].rearrange("p a n -> p (a n)"),
                                                 start=True, stop=False)
                            layers = (1,) if row.pas == 3 else (0,) if q < SQ else (0, 1)
                            opens1 = q == (SQ if row.pas == 2 else 0)
                            if opens1:
                                pe.wait_ge(comb1, (row.m - SR if row.pas == 2 else P0 + row.m) + 1)
                            multiply(*row.ring(q), c, layers, {0: False, 1: opens1}, q == row.K - 1, row.slot,
                                     wait_Y=T - QT * c if 1 in layers and is_first(i) else None)
                            for step, earlier in seg.due(i, k, q):
                                after(step, earlier)
                return body

            run_passes(pe, passes)
            for step, row in last_steps():
                after(step, row)


_INS = ['x', 'adj', 'L0_gnn_W1', 'L0_gnn_b1', 'L0_gnn_W2', 'L0_gnn_b2', 'L1_gnn_W', 'L1_gnn_b']


def kernel(**inputs):
    import numpy as _np
    import concourse.bacc as _bacc
    from concourse import mybir as _mybir
    from concourse.bass_utils import run_bass_kernel_spmd as _run

    nc = _bacc.Bacc("TRN2", target_bir_lowering=False, num_devices=1, dynamic_dma_scratch_size=1024)
    arrays, args = {}, []
    for name in _INS:
        a = _np.ascontiguousarray(inputs[name])
        arrays[f"in_{name}_dram"] = a
        args.append(nc.dram_tensor(f"in_{name}_dram", a.shape, _mybir.dt.from_np(a.dtype), kind="ExternalInput").ap())
    o = nc.dram_tensor("out_0_dram", inputs['x'].shape, _mybir.dt.float32, kind="ExternalOutput").ap()
    gnn_kernel(nc, *args, o)
    r = _run(nc, [arrays], core_ids=[0])
    return r.results[0]["out_0_dram"]
```

```python
from contextlib import ExitStack

import concourse.bass as bass
from concourse import mybir

P = 128
BL = 32
F32 = mybir.dt.float32
F32R = mybir.dt.float32r
ALU = mybir.AluOpType
ACT = mybir.ActivationFunctionType
AX = mybir.AxisListType
LN_EPS = 1e-5
TINY = 1.2e-38


def is_first(i):
    return isinstance(i, int) and i == 0


def segment(eng, trips, peel, body):
    for i in range(peel):
        body(i)
    with eng.Fori(int(peel), trips) as i:
        body(i)


def gnn_kernel(nc, x, adj, W1, b1, W2, b2, W, b, out):
    N, DF = x.shape
    HID = W1.shape[0]
    T = N // P
    KF = DF // P
    G = P // BL
    NG = N // G
    QT = 4
    QW = QT * P
    QC = QT * BL
    NQ = T // QT
    SR = 8
    SQ = SR // QT
    NB = T // SR
    RING = 4
    U1 = 4
    SLOTS = 2
    UW = HID + 2
    AHEAD = 3
    SHARED = 2

    q1 = [SR * SQ * B * (B - 1) // 2 for B in range(NB + 1)]
    P0 = T - SR

    STEPS = ("evac", "combine", "turn", "copy", "project", "finish", "norm", "y", "split")
    LAGS = {(2, 2): (1, 1, 1, 2, 2, 6, 7, 8, 8),
            (2, 4): (3, 3, 3, 5, 7, 10, 11, 12, 13),
            (2, 6): (3, 3, 3, 9, 9, 12, 12, 12, 17),
            (2, 8): (3, 3, 3, 7, 10, 13, 14, 15, 15),
            3: (4, 5, 5, 9, 9, 11, 12, 16, 16)}
    SOON = {4: (1, 1, 3, 3, 3, 3, 3, 3, 3),
            6: (2, 3, 3, 3, 3, 4, 4, 5, 5),
            8: (4, 4, 4, 4, 4, 5, 6, 7, 7)}
    BACK = 4
    PASS1 = {0: (0, 0, 0, 3, 0, 0),
             2: (1, 0, 1, 1, 0, 0),
             4: (2, 1, 1, 3, 1, 0),
             6: (1, 1, 3, 4, 1, 0)}

    def quads_of(pas, B):
        if pas == 2:
            return list(range(SQ * B, SQ * (B + 1))) + list(reversed(range(SQ * (B + 1), NQ)))
        return list(reversed(range(SQ * (B + 1))))

    class Row:

        def __init__(self, seg, i, k):
            self.seg = seg
            per = len(seg.supers)
            own = seg.supers[k % per]
            self.pas = seg.pas
            self.own = own
            self.quads = quads_of(seg.pas, own)
            self.n = seg.row0 + seg.U * i + k
            self.m = self.n - (seg.pas - 2) * T
            self.r = i * -(seg.U // per) + (SR * own + SR - 1 - k // per)
            self.slot = k % 2
            self.K = len(self.quads)
            self.before = seg.before(k)
            self.step_quads = seg.before(seg.U)
            self.q0 = seg.quad0 + self.step_quads * i + self.before
            self.turn0 = i * (self.step_quads // RING) + seg.quad0 // RING
            self.layer0 = seg.pas == 2
            self.layer1 = seg.pas == 3 or own < NB - 1
            self.part = own > 0 if seg.pas == 2 else own < NB - 1
            self.parts = seg.parts[self.slot] + seg.U // 2 * i + k // 2 + 1

        def ring(self, q):
            return self.turn0 + (self.before + q) // RING, (self.before + q) % RING

    class Segment:

        def __init__(self, pas, supers, U, last):
            self.pas, self.supers, self.U, self.last = pas, supers, U, last
            self.rows = SR * len(supers)
            self.trips = self.rows // U
            self.row0 = last.row0 + last.rows if last else 0
            self.quad0 = last.quad0 + last.trips * last.before(last.U) if last else q1[NB]
            self.parts = [0, 0]
            if last and last.pas == pas:
                with_part = [last.supers[k % len(last.supers)] < NB - 1 for k in range(2)]
                self.parts = [last.parts[k] + (last.rows // 2 if with_part[k] else 0) for k in range(2)]

        def before(self, k):
            return sum(len(quads_of(self.pas, self.supers[j % len(self.supers)])) for j in range(k))

        def row(self, i, k):
            if 0 <= k < self.U:
                return Row(self, i, k)
            if not isinstance(i, int) or i + k // self.U >= 0:
                return Row(self, i + k // self.U, k % self.U)
            return Row(self.last, *divmod(self.last.rows + self.U * i + k, self.last.U)) if self.last else None

        def due(self, i, k, q):
            serial = self.pas == 2 or self.last.pas == 2
            for d in reversed(range(1, BACK + 1)):
                row = self.row(i, k - d)
                if not row or serial and row.seg is not self and not (is_first(i) and k == 0):
                    continue
                since = sum(self.row(i, j).K for j in range(k - d + 1, k))
                lags = LAGS[3 if row.pas == 3 else (2, row.K)]
                for j, (step, lag) in enumerate(zip(STEPS, lags)):
                    if j < 2 and k - d + 1 < self.U:
                        lag = min(lag, self.row(i, k - d + 1).K)
                    if serial and row.seg is not self:
                        if lag <= since:
                            continue
                        soon = SOON[self.row(i, k).K][j] - (d - 1)
                        lag = max(min(lag, since + soon), since + 1)
                    if lag == since + q + 1:
                        yield step, row

    segments = []
    for pas, supers in ((2, (3,)), (2, (2,)), (2, (1,)), (2, (0,)), (3, (3, 0)), (3, (2, 1))):
        segments.append(Segment(pas, supers, 2 * len(supers), segments[-1] if segments else None))
    end = segments[-1]

    def last_steps():
        for q in range(max(LAGS[3])):
            yield from end.due(end.trips - 1, end.U, q)

    with ExitStack() as ctx:
        def sb(name, shape, dt=F32):
            return ctx.enter_context(nc.sbuf_tensor(name, shape, dt))

        def sem(name):
            return ctx.enter_context(nc.semaphore(name))

        with ExitStack() as early_ctx:
            rows = early_ctx.enter_context(nc.sbuf_tensor("rows", [P, U1, N], F32))
        strips = sb("strips", [P, SLOTS, N])
        Y = sb("Y", [P, T, 2, DF], F32R)
        xs = sb("xs", [P, T, DF])
        U = sb("U", [P, T, 2, UW], F32R)
        part0 = sb("part0", [P, P0, UW])
        tq = sb("tq", [P, RING, QW])
        hi = sb("hi", [P, RING, QW], F32R)
        lo = sb("lo", [P, RING, QW], F32R)
        ident = sb("ident", [P, P])
        ident_r = sb("ident_r", [P, P], F32R)
        W1T = sb("W1T", [P, KF, HID])
        W2T = sb("W2T", [P, DF])
        Wm = sb("Wm", [P, KF, DF])
        b1_all = sb("b1_all", [P, HID])
        b2_all = sb("b2_all", [P, DF])
        b_all = sb("b_all", [P, DF])
        d21 = sb("d21", [P, T * 2])
        expo = sb("expo", [P, T])
        sums = sb("sums", [P, U1, G])
        pick = sb("pick", [P, (2 * G - 1) * BL])
        degree = sb("degree", [P, 2, 2])
        loop = sb("loop", [P, 2])
        stats = sb("stats", [P, 2, 6])
        mv = sb("mv", [P, 2, 2])
        stats_x = sb("stats_x", [P, T, 6])
        mv_x = sb("mv_x", [P, T, 2])
        ln_x = sb("ln_x", [P, 4, T])
        power = sb("power", [P, 2])
        mask = sb("mask", [P, 2])
        rstd = sb("rstd", [P, 4])
        ln_scale = sb("ln_scale", [P, 2])
        ln_bias = sb("ln_bias", [P, 2])
        h = sb("h", [P, 2, DF])
        colT = sb("colT", [P, 2, DF])
        w_in = colT
        ut = sb("ut", [P, 2, HID + 1])
        us = sb("us", [P, 2, UW])
        accb0 = sb("accb0", [P, 2, UW])
        accb1 = sb("accb1", [P, 2, DF])
        agg = sb("agg", [P, 2, DF])
        stage = sb("stage", [P, 2, DF])
        part1 = sb("part1", [P, 2, DF])
        spill = nc.dram_tensor("spill", (P0, P, DF), F32).ap()

        ps = ctx.enter_context(nc.psum_tensor("ps", [P, 8, 512], F32))

        def acc0(k):
            return ps[:, k, :]

        def acc1(k):
            return ps[:, 2 + k, :]

        def acc_sum(k):
            return acc0(k)[:, HID + 1:HID + 2]

        def fin(k):
            return ps[:, 4 + k, :]

        const_in = sem("const_in")
        x_in = [sem(f"x_in{B}") for B in range(NB)]
        ident_ok = sem("ident_ok")
        ident_r_ok = sem("ident_r_ok")
        wT_ps = sem("wT_ps")
        wT_ok = sem("wT_ok")
        row_in = [sem(f"row_in{i}") for i in range(U1)]
        strip_in = [sem(f"strip_in{i}") for i in range(SLOTS)]
        pick_ok = sem("pick_ok")
        sum_act = sem("sum_act")
        sum_dve = sem("sum_dve")
        sum_ps = sem("sum_ps")
        sum_ok = sem("sum_ok")
        x_stats = sem("x_stats")
        stats_ok = sem("stats_ok")
        ln_ok = sem("ln_ok")
        h_ok = sem("h_ok")
        hT_ps = sem("hT_ps")
        hT_ok = sem("hT_ok")
        u_ps = sem("u_ps")
        u_read = sem("u_read")
        deg_ok = sem("deg_ok")
        U_ok = sem("U_ok")
        quad_T = sem("quad_T")
        row_T = sem("row_T")
        hi_ok = sem("hi_ok")
        lo_ok = sem("lo_ok")
        lo_pool = sem("lo_pool")
        quad_M = sem("quad_M")
        accb0_ok = sem("accb0_ok")
        accb1_ok = sem("accb1_ok")
        comb0 = sem("comb0")
        comb1 = sem("comb1")
        agg_ok = sem("agg_ok")
        agg_ps = sem("agg_ps")
        aggT_ok = sem("aggT_ok")
        fin_ps = sem("fin_ps")
        fin_read = sem("fin_read")
        Y_ok = sem("Y_ok")
        stage_ok = sem("stage_ok")
        stage_st = [sem(f"stage_st{i}") for i in range(2)]
        part1_in = [sem(f"part1_in{i}") for i in range(2)]
        dve_step = sem("dve_step")
        x_b2 = sem("x_b2")
        x1_stats = sem("x1_stats")
        pool_step = sem("pool_step")
        ln_step = sem("ln_step")
        waited = sem("waited")

        block = ctx.enter_context(nc.Block())

        def d1_of(r):
            return d21[:, bass.ds(r * 2 + 1, 1)]

        def d2_of(r):
            return d21[:, bass.ds(r * 2, 1)]

        def wait_apart(eng, s, n):
            eng.wait_ge(s, n)
            eng.sem_inc(waited, 1)

        adj_blocks = adj.rearrange("(g t k) (h c) -> t g h k c", g=G, k=BL, h=G)
        out_rows = out.rearrange("(g t k) f -> t g k f", g=G, k=BL)

        def sums_by_act(r):
            few = isinstance(r, int) and r <= SHARED * SR
            return 1 + ((G - 1) * r if few else G * r - SHARED * SR)

        def by_pool(j):
            return j % 2 == 1

        def lower_made(g, j):
            return (lo_pool if by_pool(j) else lo_ok), RING // 2 * g + (RING // 2 + j // 2 + 1)

        def ring1(B, i, s, q):
            K = SQ * B
            return i * (U1 * K // RING) + (q1[B] // RING + (s * K + q) // RING), (s * K + q) % RING

        def run_passes(eng, passes):
            for seg in segments:
                segment(eng, seg.trips, 2 if seg.pas == 2 else 1, passes(seg))

        @block.sync
        def _(sp):
            sp.dma_start(w_in[:, 0, :], W1).then_inc(const_in, 16)
            sp.dma_start(w_in[:, 1, :].rearrange("p (k h) -> p k h", k=KF),
                         W2.rearrange("(k p) h -> p k h", p=P)).then_inc(const_in, 16)

            def load_row(r, s):
                for g in range(G):
                    sp.dma_start(rows[:, s, g * NG:(g + 1) * NG], adj_blocks[r, g]).then_inc(row_in[s], 16)

            x_tiles = x.rearrange("(g t k) f -> g k t f", g=G, k=BL)

            def load_x(B):
                for g in range(G):
                    sp.dma_start(xs[g * BL:(g + 1) * BL, SR * B:SR * (B + 1), :],
                                 x_tiles[g][:, SR * B:SR * (B + 1), :]).then_inc(x_in[B], 16)

            load_x(0)
            for dst, src, s in ((b1_all, b1, stage_st[0]), (b2_all, b2, stage_st[1]), (b_all, b, const_in)):
                sp.dma_start(dst[:, :], src.rearrange("(a n) -> a n", a=1).to_broadcast([P, src.shape[0]])
                             ).then_inc(s, 16)
            sp.dma_start(Wm[:, :, :], W.rearrange("(k p) f -> p k f", p=P)).then_inc(const_in, 16)

            load_row(0, 0)
            for s in range(1, U1):
                load_row(s, s)
                load_x(s)

            def next_rows(transposed):
                def body(i):
                    for s in range(U1):
                        r = U1 * i + s
                        wait_apart(sp, sum_act, sums_by_act(r - U1 + 1))
                        if isinstance(r, int) and r - U1 < SHARED * SR:
                            sp.wait_ge(sum_dve, r - U1 + 1)
                        if transposed:
                            wait_apart(sp, row_T, r - U1 - SR + 1)
                        load_row(r, s)
                return body

            for i in range(1, 5):
                next_rows(i > 2)(i)
            with sp.Fori(5, T // U1) as i:
                next_rows(True)(i)

            def load_strip(row):
                a, z = (SQ * row.own * QC, NG) if row.pas == 2 else (0, SQ * (row.own + 1) * QC)
                for g in range(G):
                    sp.dma_start(strips[:, row.slot, g * NG + a:g * NG + z],
                                 adj_blocks[row.r, g][:, :, a:z]).then_inc(strip_in[row.slot], 16)

            def load_part1(row):
                wait_apart(sp, agg_ok, row.n - 1)
                sp.dma_start(part1[:, row.slot, :], spill[row.r]).then_inc(part1_in[row.slot], 16)

            def passes(seg):
                def body(i):
                    for k in range(seg.U):
                        row, last = seg.row(i, k), seg.row(i, k - 1)
                        if isinstance(row.n, int) and row.n < SLOTS:
                            wait_apart(sp, sum_act, sums_by_act(T - U1 + k + 1))
                            wait_apart(sp, row_T, P0 - U1 + k + 1)
                        else:
                            wait_apart(sp, row_T, P0 + row.n - SLOTS + 1)
                        load_strip(row)
                        if last and last.pas == 3 and last.part:
                            load_part1(last)
                return body

            run_passes(sp, passes)
            load_part1(end.row(end.trips - 1, end.U - 1))
            for k in range(SLOTS):
                sp.wait_ge(stage_st[k], 16 + 16 * (P0 + T) // 2)

        @block.gpsimd
        def _(pool):
            nc.gpsimd.memset(expo[:, :], -0.5)
            nc.gpsimd.memset(ident[:, :], 0.0).then_inc(pool_step, 1)
            pool.wait_ge(pool_step, 1)
            nc.gpsimd.affine_select(out=ident[:, :], in_=ident[:, :], compare_op=ALU.not_equal, fill=1.0,
                                    base=0, pattern=[[-1, P]], channel_multiplier=1).then_inc(ident_ok, 1)
            pool.wait_ge(ident_ok, 1)
            nc.gpsimd.tensor_copy(ident_r[:, :], ident[:, :]).then_inc(ident_r_ok, 1)
            pool.sem_inc(Y_ok, 2)

            class Steps:

                def __init__(self, n, counter=pool_step):
                    self.n, self.counter = n, counter

                def __call__(self, ins):
                    ins.then_inc(self.counter, 1)
                    self.n = self.n + 1
                    wait_apart(pool, self.counter, self.n)

            def norm_x(B):
                step = Steps(2 * B, ln_step)
                t = slice(SR * B, SR * (B + 1))
                pool.wait_ge(stats_ok, SR * (B + 1))
                nc.gpsimd.tensor_scalar(ln_x[:, 2, t], mv_x[:, t, 0], -1.0, None, ALU.mult)
                step(nc.gpsimd.tensor_scalar(ln_x[:, 0, t], mv_x[:, t, 1], LN_EPS, None, ALU.add))
                step(nc.gpsimd.tensor_tensor(ln_x[:, 1, t], ln_x[:, 0, t], expo[:, t], ALU.pow))
                nc.gpsimd.tensor_tensor(ln_x[:, 3, t], ln_x[:, 2, t], ln_x[:, 1, t], ALU.mult
                                        ).then_inc(ln_ok, 1)

            def lower(g, j):
                if not by_pool(j):
                    return
                pool.wait_ge(hi_ok, RING * g + j + 1)
                nc.gpsimd.tensor_tensor(lo[:, j, :], tq[:, j, :], hi[:, j, :].bitcast(F32), ALU.subtract
                                        ).then_inc(lo_pool, 1)

            def degrees(r, s):
                step = Steps(1 + STEPS1 * r)
                wait_apart(pool, sum_ok, r + 1)
                k = s % 2
                nc.gpsimd.tensor_scalar(mask[:, :], degree[:, k, :], TINY, None, ALU.is_gt)
                step(nc.gpsimd.tensor_tensor(power[:, :], degree[:, k, :], expo[:, 0:2], ALU.pow))
                nc.gpsimd.tensor_tensor(d21[:, bass.ds(r * 2, 2)], power[:, :], mask[:, :], ALU.mult
                                        ).then_inc(deg_ok, 1)

            STEPS1, STEPS2 = 1, 3

            def pass1(B):
                K = SQ * B
                _, _, powers_at, _, _, _ = PASS1[K]

                def body(i):
                    for s in range(U1):
                        r = SR * B + U1 * i + s
                        for q in range(max(K, 1)):
                            if K:
                                lower(*ring1(B, i, s, q))
                            if q == powers_at and not (isinstance(r, int) and r == 0):
                                degrees(r - 1, s - 1)
                        if B == 0 and r % 2 == 0:
                            norm_x(r // 2)
                return body

            for B in range(NB):
                segment(pool, SR // U1, B == 0, pass1(B))
            degrees(T - 1, U1 - 1)
            pool.wait_ge(deg_ok, T)

            def after(step_name, row):
                if row.pas == 3:
                    return
                k, m, r = row.slot, row.m, row.r
                if step_name == "norm":
                    step = Steps(1 + STEPS1 * T + STEPS2 * m)
                    wait_apart(pool, stats_ok, T + m + 1)
                    step(nc.gpsimd.tensor_scalar(rstd[:, 0:1], mv[:, k, 1:2], LN_EPS, None, ALU.add))
                    step(nc.gpsimd.tensor_tensor(rstd[:, 1:2], rstd[:, 0:1], expo[:, 0:1], ALU.pow))
                    step(nc.gpsimd.tensor_tensor(ln_scale[:, k:k + 1], rstd[:, 1:2], d2_of(r),
                                                 ALU.mult))
                    nc.gpsimd.tensor_scalar(ln_bias[:, k:k + 1], mv[:, k, 0:1], ln_scale[:, k:k + 1], -1.0,
                                            ALU.mult, ALU.mult).then_inc(ln_ok, 1)
                if step_name == "split":
                    wait_apart(pool, h_ok, T + m + 1)
                    nc.gpsimd.tensor_tensor(Y[:, r, 1, :], h[:, k, :], Y[:, r, 0, :].bitcast(F32),
                                            ALU.subtract).then_inc(Y_ok, 1)

            def passes(seg):
                def body(i):
                    for k in range(seg.U):
                        row = seg.row(i, k)
                        for q in range(row.K):
                            lower(*row.ring(q))
                            for step, earlier in seg.due(i, k, q):
                                after(step, earlier)
                return body

            run_passes(pool, passes)

        @block.scalar
        def _(act):
            act.sem_inc(sum_act, 1)
            act.wait_ge(wT_ps, 1)
            nc.scalar.activation(W1T[:, :, :].rearrange("p k h -> p (k h)"), ps[:, 0, 0:KF * HID], ACT.Copy)
            nc.scalar.activation(W2T[:, :], ps[:, 1, 0:DF], ACT.Copy).then_inc(wT_ok, 1)

            def upper(g, j):
                act.wait_ge(quad_T, RING * g + j + 1)
                act.wait_ge(quad_M, RING * g + j + 1)
                nc.scalar.activation(hi[:, j, :], tq[:, j, :], ACT.Copy).then_inc(hi_ok, 1)

            def evac0(e, r, k):
                act.wait_ge(comb0, e + 1)
                nc.scalar.activation(accb0[:, k, :], acc0(k)[:, UW:2 * UW], ACT.Copy,
                                     scale=d1_of(r)).then_inc(accb0_ok, 1)

            def evac1(f, r, k, done):
                act.wait_ge(quad_M, RING + done)
                act.wait_ge(comb1, f + 1)
                nc.scalar.activation(accb1[:, k, :], acc1(k)[:, DF:2 * DF], ACT.Copy,
                                     scale=d2_of(r)).then_inc(accb1_ok, 1)

            def pass1(B):
                K = SQ * B
                _, _, _, copy_at, evac_at, _ = PASS1[K]

                def body(i):
                    for s in range(U1):
                        r = SR * B + U1 * i + s
                        groups = G if B >= SHARED else G - 1
                        if B:
                            make_h(r, s % 2)
                        act.wait_ge(row_in[s], 16 * G * (SR // U1 * B + i + 1))
                        for q in range(max(K, G)):
                            if q < groups:
                                act.wait_ge(sum_act, sums_by_act(r) + q)
                                nc.scalar.activation(
                                    ps[:, 4:6, :].rearrange("p a n -> p (a n)")[:, K * QC:NG],
                                    rows[:, s, q * NG + K * QC:(q + 1) * NG],
                                    ACT.Copy, accum_out=sums[:, s, q:q + 1]).then_inc(sum_act, 1)
                            if q < K:
                                upper(*ring1(B, i, s, q))
                            if B == 0 and q == 1:
                                make_h(r, s % 2)
                            if q == copy_at:
                                act.wait_ge(hT_ps, r + 1)
                                nc.scalar.activation(colT[:, s % 2, :], ps[:, 2 + s % 2, 0:DF], ACT.Copy
                                                     ).then_inc(hT_ok, 1)
                            if q == evac_at and B and not (B == 1 and is_first(i) and s < 2):
                                act.wait_ge(deg_ok, r - 1)
                                evac0(r - 2 - SR, r - 2, s % 2)
                return body

            def make_h(r, k):
                nc.scalar.activation(h[:, k, :], xs[:, r, :], ACT.Relu, bias=ln_x[:, 3, bass.ds(r, 1)],
                                     scale=ln_x[:, 1, bass.ds(r, 1)]).then_inc(h_ok, 1)

            for B in range(NB):
                act.wait_ge(ln_ok, B + 1)
                segment(act, SR // U1, B < 2, pass1(B))
            for r in (T - 2, T - 1):
                act.wait_ge(deg_ok, r + 1)
                evac0(r - SR, r, r % 2)

            def after(step, row):
                k, m, r = row.slot, row.m, row.r
                if step == "evac":
                    if row.layer0:
                        act.wait_ge(quad_M, RING + row.q0 + row.K)
                        evac0(P0 + m, r, k)
                    if row.layer1:
                        evac1(m - SR if row.pas == 2 else P0 + m, r, k, row.q0 + row.K)
                if step == "copy":
                    w = HID if row.layer0 else DF
                    act.wait_ge(agg_ps, row.n + 1)
                    nc.scalar.activation(colT[:, k, 0:w], fin(k)[:, 0:w], ACT.Copy).then_inc(aggT_ok, 1)
                    if row.layer0 and row.layer1:
                        wait_apart(act, stage_ok, m - SR + 1)
                        act.dma_start(spill[r], stage[:, k, :]).then_inc(stage_st[k], 16)
                if step == "y" and row.pas == 2:
                    act.wait_ge(ln_ok, NB + m + 1)
                    act.wait_ge(Y_ok, m + 1)
                    for dst in (h[:, k, :], Y[:, r, 0, :]):
                        last = nc.scalar.activation(dst, xs[:, r, :], ACT.Relu, bias=ln_bias[:, k:k + 1],
                                                    scale=ln_scale[:, k:k + 1])
                    last.then_inc(h_ok, 1)
                if step == "y" and row.pas == 3:
                    wait_apart(act, stage_ok, P0 + m + 1)
                    act.dma_start(out_rows[r], stage[:, k, :]).then_inc(stage_st[k], 16)

            def passes(seg):
                def body(i):
                    for k in range(seg.U):
                        row = seg.row(i, k)
                        for q in range(row.K):
                            upper(*row.ring(q))
                            for step, earlier in seg.due(i, k, q):
                                after(step, earlier)
                return body

            run_passes(act, passes)
            for step, row in last_steps():
                after(step, row)

        @block.vector
        def _(dve):
            nc.vector.memset(ut[:, :, HID:HID + 1], 1.0).then_inc(dve_step, 1)
            nc.vector.memset(us[:, :, HID + 1:UW], 1.0).then_inc(dve_step, 1)
            dve.wait_ge(dve_step, 2)
            for s, n in ((lo_ok, 2), (lo_pool, 2), (comb0, 2), (comb1, 2), (u_read, 2), (fin_read, 2)):
                dve.sem_inc(s, n)
            nc.vector.memset(loop[:, 0:1], 0.0)
            nc.vector.memset(loop[:, 1:2], 1.0)
            nc.vector.memset(pick[:, :], 0.0).then_inc(dve_step, 1)
            dve.wait_ge(dve_step, 3)
            dve.wait_ge(ident_ok, 1)
            nc.vector.tensor_reduce(pick[:, (G - 1) * BL:G * BL], ident[:, :].rearrange("p (h k) -> p k h", h=G),
                                    AX.X, ALU.add).then_inc(pick_ok, 1)
            dve.wait_ge(const_in, 64)
            dve.wait_ge(stage_st[0], 16)
            dve.wait_ge(stage_st[1], 16)

            def stats_of_x(B):
                dve.wait_ge(x_in[B], 16 * G)
                for t in range(SR * B, SR * (B + 1)):
                    nc.vector.bn_stats(stats_x[:, t, :], xs[:, t, :]).then_inc(x_stats, 1)
                dve.wait_ge(x_stats, SR * (B + 1))
                for t in range(SR * B, SR * (B + 1)):
                    nc.vector.bn_aggr(mv_x[:, t, :], stats_x[:, t, :]).then_inc(stats_ok, 1)

            stats_of_x(0)
            STEPS1 = 2
            base1 = 3

            def turn(turn_slot, src, c):
                g, j = turn_slot
                dve.wait_ge(*lower_made(g - 1, j))
                blocks = src.rearrange("p (g t c) -> p g t c", g=G, c=BL)
                dst = tq[:, j, :].rearrange("p (t g c) -> p g t c", t=QT, g=G)
                nc.vector.transpose(dst, blocks[:, :, c * QT:(c + 1) * QT, :]).then_inc(quad_T, 1)

            def row_free(n):
                dve.wait_ge(quad_T, n)
                dve.sem_inc(row_T, 1)

            def lower(g, j):
                if by_pool(j):
                    return
                dve.wait_ge(hi_ok, RING * g + j + 1)
                nc.vector.tensor_tensor(lo[:, j, :], tq[:, j, :], hi[:, j, :].bitcast(F32),
                                        ALU.subtract).then_inc(lo_ok, 1)

            def combine0(e, r, k, dst):
                dve.wait_ge(accb0_ok, e + 1)
                nc.vector.scalar_tensor_tensor(out=dst, in0=acc0(k)[:, 0:UW], scalar=d1_of(r),
                                               in1=accb0[:, k, :], op0=ALU.mult, op1=ALU.add
                                               ).then_inc(comb0, 1)

            def combine1(f, r, k, dst):
                dve.wait_ge(accb1_ok, f + 1)
                nc.vector.scalar_tensor_tensor(out=dst, in0=acc1(k)[:, 0:DF], scalar=d2_of(r),
                                               in1=accb1[:, k, :], op0=ALU.mult, op1=ALU.add
                                               ).then_inc(comb1, 1)

            def make_U(r, k):
                at = base1 + STEPS1 * r
                dve.wait_ge(u_ps, r + 1)
                nc.vector.tensor_tensor(ut[:, k, 0:HID], ps[:, 2 + k, DF:DF + HID], b1_all[:, :], ALU.add
                                        ).then_inc(u_read, 1)
                dve.wait_ge(u_read, 2 + r + 1)
                dve.wait_ge(deg_ok, r + 1)
                nc.vector.tensor_scalar(us[:, k, 0:HID + 1], ut[:, k, :], d1_of(r), None, ALU.mult
                                        ).then_inc(dve_step, 1)
                dve.wait_ge(dve_step, at + 1)
                nc.vector.tensor_copy(U[:, r, 0, :], us[:, k, :]).then_inc(dve_step, 1)
                dve.wait_ge(dve_step, at + 2)
                nc.vector.tensor_tensor(U[:, r, 1, :], us[:, k, :], U[:, r, 0, :].bitcast(F32),
                                        ALU.subtract).then_inc(U_ok, 1)

            def pass1(B):
                K = SQ * B
                degree_at, u_at, _, _, _, combine_at = PASS1[K]

                def body(i):
                    for s in range(U1):
                        r = SR * B + U1 * i + s
                        n0 = q1[B] + (U1 * i + s) * K

                        def quad(q):
                            return ring1(B, i, s, q)

                        if K:
                            dve.wait_ge(row_in[s], 16 * G * (SR // U1 * B + i + 1))
                        for q in range(min(AHEAD, K)):
                            turn(quad(q), rows[:, s, :], q)
                        last = max(K, 1) - 1
                        edge = is_first(i) and B and s == 0
                        for q in range(last + 1):
                            if K:
                                lower(*quad(q))
                            if q + AHEAD < K:
                                turn(quad(q + AHEAD), rows[:, s, :], q + AHEAD)
                            if q == K - 1:
                                row_free(n0 + K)
                            if q == u_at and not (is_first(i) and s == 1) and not (B == 0 and r < 2):
                                make_U(r - 2, s % 2)
                            if q == combine_at and B and not (B == 1 and is_first(i) and s < 2):
                                combine0(r - 2 - SR, r - 2, s % 2, part0[:, r - 2 - SR, :])
                            if q == degree_at and not (isinstance(r, int) and r == 0):
                                row_sum(r - 1, s - 1)
                            if q == last and edge:
                                make_U(r - 1, (s - 1) % 2)
                        if B < SHARED:
                            dve.wait_ge(row_in[s], 16 * G * (SR // U1 * B + i + 1))
                            nc.vector.tensor_reduce(sums[:, s, G - 1:G],
                                                    rows[:, s, (G - 1) * NG + K * QC:N], AX.X, ALU.add
                                                    ).then_inc(sum_dve, 1)
                        if B == 0 and r % 2 == 1 and r < 2 * NB - 2:
                            stats_of_x((r + 1) // 2)
                return body

            def row_sum(r, s):
                dve.wait_ge(sum_ps, r + 1)
                nc.vector.tensor_scalar(degree[:, s % 2, :], loop[:, :], acc_sum(s % 2), TINY, ALU.add, ALU.max
                                        ).then_inc(sum_ok, 1)

            for B in range(NB):
                segment(dve, SR // U1, True, pass1(B))
            make_U(T - 2, 0)
            row_sum(T - 1, 1)
            make_U(T - 1, 1)
            for r in (T - 2, T - 1):
                combine0(r - SR, r, r % 2, part0[:, r - SR, :])

            def after(step, row):
                k, m, r = row.slot, row.m, row.r
                if step == "combine" and row.pas == 2:
                    combine0(P0 + m, r, k, us[:, k, :] if row.part else agg[:, k, 0:UW])
                    dve.wait_ge(comb0, 2 + P0 + m + 1)
                    if row.part:
                        nc.vector.tensor_tensor(agg[:, k, 0:UW], us[:, k, :], part0[:, r - SR, :], ALU.add
                                                ).then_inc(agg_ok, 1)
                    else:
                        dve.sem_inc(agg_ok, 1)
                    if row.layer1:
                        wait_stage(m - SR, k)
                        combine1(m - SR, r, k, stage[:, k, :])
                        dve.wait_ge(comb1, 2 + m - SR + 1)
                        dve.sem_inc(stage_ok, 1)
                    dve.wait_ge(agg_ok, row.n + 1)
                    nc.vector.scalar_tensor_tensor(out=xs[:, r, :], in0=b2_all[:, :],
                                                   scalar=agg[:, k, HID:HID + 1], in1=xs[:, r, :],
                                                   op0=ALU.mult, op1=ALU.add).then_inc(x_b2, 1)
                if step == "combine" and row.pas == 3:
                    combine1(P0 + m, r, k, h[:, k, :] if row.part else agg[:, k, :])
                    dve.wait_ge(comb1, 2 + P0 + m + 1)
                    if row.part:
                        dve.wait_ge(part1_in[k], 16 * row.parts)
                        nc.vector.tensor_tensor(agg[:, k, :], h[:, k, :], part1[:, k, :], ALU.add
                                                ).then_inc(agg_ok, 1)
                    else:
                        dve.sem_inc(agg_ok, 1)
                if step == "finish":
                    if row.pas == 2:
                        dve.wait_ge(x_b2, m + 1)
                    dve.wait_ge(fin_ps, row.n + 1)
                    if row.pas == 2:
                        nc.vector.tensor_tensor(xs[:, r, :], xs[:, r, :], fin(k)[:, DF:2 * DF], ALU.add
                                                ).then_inc(fin_read, 1)
                        wait_apart(dve, fin_read, 2 + row.n + 1)
                        nc.vector.bn_stats(stats[:, k, :], xs[:, r, :]).then_inc(x1_stats, 1)
                        dve.wait_ge(x1_stats, m + 1)
                        wait_apart(dve, ln_ok, NB + m - 1)
                        nc.vector.bn_aggr(mv[:, k, :], stats[:, k, :]).then_inc(stats_ok, 1)
                    else:
                        wait_stage(P0 + m, k)
                        nc.vector.tensor_tensor(stage[:, k, :], fin(k)[:, DF:2 * DF], b_all[:, :], ALU.add
                                                ).then_inc(fin_read, 1)
                        dve.wait_ge(fin_read, 2 + row.n + 1)
                        nc.vector.scalar_tensor_tensor(out=stage[:, k, :], in0=stage[:, k, :], scalar=0.0,
                                                       in1=xs[:, r, :], op0=ALU.max, op1=ALU.add
                                                       ).then_inc(stage_ok, 1)

            def wait_stage(f, k):
                dve.wait_ge(stage_st[k], 8 * (f - k) + 16)

            def passes(seg):
                def body(i):
                    for k in range(seg.U):
                        row = seg.row(i, k)
                        source = strips[:, row.slot, :]
                        dve.wait_ge(strip_in[row.slot], (row.n - row.slot) * (8 * G) + 16 * G)
                        for q in range(min(AHEAD, row.K)):
                            turn(row.ring(q), source, row.quads[q])
                        for q in range(row.K):
                            lower(*row.ring(q))
                            if q + AHEAD < row.K:
                                turn(row.ring(q + AHEAD), source, row.quads[q + AHEAD])
                            if q == row.K - 2:
                                row_free(row.q0 + row.K)
                            for step, earlier in seg.due(i, k, q):
                                after(step, earlier)
                return body

            run_passes(dve, passes)
            for step, row in last_steps():
                after(step, row)

        @block.tensor
        def _(pe):
            pe.sem_inc(quad_M, RING)
            pe.wait_ge(ident_ok, 1)
            pe.wait_ge(ident_r_ok, 1)
            pe.wait_ge(pick_ok, 1)
            pe.wait_ge(const_in, 64)
            for f in range(KF):
                nc.tensor.transpose(ps[:, 0, f * P:(f + 1) * P], w_in[:, 0, f * P:(f + 1) * P], ident[:, :])
                last = nc.tensor.transpose(ps[:, 1, f * P:(f + 1) * P], w_in[:, 1, f * P:(f + 1) * P],
                                           ident[:, :])
            last.then_inc(wT_ps, 1)
            pe.wait_ge(wT_ok, 1)

            def multiply(turn_slot, c, layers, opens, closes, k, wait_Y=None, wait_U=None):
                slot = turn_slot[1]
                pe.wait_ge(*lower_made(*turn_slot))
                if wait_Y is not None:
                    pe.wait_ge(Y_ok, 2 + wait_Y)
                if wait_U is not None:
                    pe.wait_ge(U_ok, wait_U)
                for j in range(QT):
                    t = c * QT + j
                    a_hi = hi[:, slot, j * P:(j + 1) * P]
                    a_lo = lo[:, slot, j * P:(j + 1) * P]
                    for layer in layers:
                        right, w, a = (U, UW, acc0(k)) if layer == 0 else (Y, DF, acc1(k))
                        last = nc.tensor.matmul(a[:, 0:2 * w], a_hi,
                                                right[:, t, :, :].rearrange("p a n -> p (a n)"),
                                                start=opens[layer] and j == 0, stop=False)
                    for layer in layers:
                        right, w, a = (U, UW, acc0(k)) if layer == 0 else (Y, DF, acc1(k))
                        last = nc.tensor.matmul(a[:, 0:w], a_lo, right[:, t, 0, :], start=False,
                                                stop=closes and j == QT - 1)
                last.then_inc(quad_M, 1)

            def pass1(B):
                K = SQ * B

                def body(i):
                    for s in range(U1):
                        r = SR * B + U1 * i + s
                        if not (isinstance(r, int) and r == 0):
                            before(r - 1, s - 1, opens=B == 0 or B == 1 and is_first(i) and s == 0)
                        pe.wait_ge(h_ok, r + 1)
                        pe.wait_ge(u_read, r + 1)
                        for f in range(KF):
                            last = nc.tensor.transpose(ps[:, 2 + s % 2, f * P:(f + 1) * P],
                                                       h[:, s % 2, f * P:(f + 1) * P], ident[:, :])
                        last.then_inc(hT_ps, 1)
                        for q in range(K):
                            if q == 0:
                                pe.wait_ge(comb0, r - SR + 1)
                            multiply(ring1(B, i, s, q), q, (0,), {0: q == 0}, False,
                                     s % 2, wait_U=QT * (q + 1) if is_first(i) else None)
                return body

            def before(r, s, opens=False):
                pe.wait_ge(hT_ok, r + 1)
                for f in range(KF):
                    last = nc.tensor.matmul(ps[:, 2 + s % 2, DF:DF + HID], colT[:, s % 2, f * P:(f + 1) * P],
                                            W1T[:, f, :], start=f == 0, stop=f == KF - 1)
                last.then_inc(u_ps, 1)
                pe.wait_ge(sum_act, sums_by_act(r + 1))
                if isinstance(r, int) and r < SHARED * SR:
                    pe.wait_ge(sum_dve, r + 1)
                for g in range(G):
                    z = (G - 1 - g) * BL
                    last = nc.tensor.matmul(acc_sum(s % 2), pick[:, z:z + P], sums[:, s % U1, g:g + 1],
                                            start=opens and g == 0, stop=g == G - 1)
                last.then_inc(sum_ps, 1)

            for B in range(NB):
                segment(pe, SR // U1, True, pass1(B))
            before(T - 1, U1 - 1)
            pe.wait_ge(U_ok, T)

            def after(step, row):
                k = row.slot
                if step == "turn":
                    pe.wait_ge(agg_ok, row.n + 1)
                    pe.wait_ge(fin_read, row.n + 1)
                    for f in range((HID if row.layer0 else DF) // P):
                        last = nc.tensor.transpose(fin(k)[:, f * P:(f + 1) * P],
                                                   agg[:, k, f * P:(f + 1) * P], ident[:, :])
                    last.then_inc(agg_ps, 1)
                if step == "project":
                    pe.wait_ge(aggT_ok, row.n + 1)
                    if row.layer0:
                        last = nc.tensor.matmul(fin(k)[:, DF:2 * DF], colT[:, k, 0:HID], W2T[:, :],
                                                start=True, stop=True)
                    else:
                        for f in range(KF):
                            last = nc.tensor.matmul(fin(k)[:, DF:2 * DF], colT[:, k, f * P:(f + 1) * P],
                                                    Wm[:, f, :], start=f == 0, stop=f == KF - 1)
                    last.then_inc(fin_ps, 1)

            def passes(seg):
                def body(i):
                    for k in range(seg.U):
                        row = seg.row(i, k)
                        for q, c in enumerate(row.quads):
                            if row.layer0 and q == 0:
                                pe.wait_ge(comb0, P0 + row.m + 1)
                                nc.tensor.matmul(acc0(row.slot)[:, 0:2 * UW], ident_r[:, :],
                                                 U[:, row.r, :, :].rearrange("p a n -> p (a n)"),
                                                 start=True, stop=False)
                            layers = (1,) if row.pas == 3 else (0,) if q < SQ else (0, 1)
                            opens1 = q == (SQ if row.pas == 2 else 0)
                            if opens1:
                                pe.wait_ge(comb1, (row.m - SR if row.pas == 2 else P0 + row.m) + 1)
                            multiply(row.ring(q), c, layers, {0: False, 1: opens1}, q == row.K - 1, row.slot,
                                     wait_Y=T - QT * c if 1 in layers and is_first(i) else None)
                            for step, earlier in seg.due(i, k, q):
                                after(step, earlier)
                return body

            run_passes(pe, passes)
            for step, row in last_steps():
                after(step, row)


_INS = ['x', 'adj', 'L0_gnn_W1', 'L0_gnn_b1', 'L0_gnn_W2', 'L0_gnn_b2', 'L1_gnn_W', 'L1_gnn_b']


def kernel(**inputs):
    import numpy as _np
    import concourse.bacc as _bacc
    from concourse import mybir as _mybir
    from concourse.bass_utils import run_bass_kernel_spmd as _run

    nc = _bacc.Bacc("TRN2", target_bir_lowering=False, num_devices=1, dynamic_dma_scratch_size=1024)
    arrays, args = {}, []
    for name in _INS:
        a = _np.ascontiguousarray(inputs[name])
        arrays[f"in_{name}_dram"] = a
        args.append(nc.dram_tensor(f"in_{name}_dram", a.shape, _mybir.dt.from_np(a.dtype), kind="ExternalInput").ap())
    o = nc.dram_tensor("out_0_dram", inputs['x'].shape, _mybir.dt.float32, kind="ExternalOutput").ap()
    gnn_kernel(nc, *args, o)
    r = _run(nc, [arrays], core_ids=[0])
    return r.results[0]["out_0_dram"]
```
